# Optimizing a Trainium2 kernel written in Bass

```python
import numpy as np
import jax
import jax.numpy as jnp

def _softmax(x, axis=-1):
    return jax.nn.softmax(x, axis=axis)

def _gelu(x):
    return jax.nn.gelu(x, approximate=True)

def _silu(x):
    return jax.nn.silu(x)

def _sigmoid(x):
    return jax.nn.sigmoid(x)

def _layernorm(x, axis=-1, eps=1e-05):
    m = jnp.mean(x, axis=axis, keepdims=True)
    v = jnp.var(x, axis=axis, keepdims=True)
    return (x - m) / jnp.sqrt(v + eps)

def _scatter_add(tgt, idx, src, axis=0):
    return tgt.at[idx].add(src)

def _segment_sum(src, seg, n):
    return jax.ops.segment_sum(src, seg, n)
kernel_name = 'mk_gps_d1_gnn_r8_894e48'

def setup_inputs(seed: int=0):
    np.random.seed(seed)
    _w = jnp.asarray

    def _rec_inputs():
        import jax
        import jax.numpy as jnp
        _gk = jax.random.key(seed)
        x = -0.0002117 + 1 * jax.random.normal(jax.random.fold_in(_gk, 1), (12500, 256), jnp.float32)
        _s = jax.random.randint(jax.random.fold_in(_gk, 2), (100000,), 0, 12500, jnp.int32)
        _d = jax.random.randint(jax.random.fold_in(_gk, 3), (100000,), 0, 12500, jnp.int32)
        _loop = jnp.arange(12500, dtype=jnp.int32)
        src = jnp.concatenate([_s, _d, _loop])
        dst = jnp.concatenate([_d, _s, _loop])
        _o = jnp.argsort(dst, stable=True)
        src = src[_o]
        dst = dst[_o]
        return (x, src, dst)
    x, src, dst = _rec_inputs()

    def _L0_gnn_setup():
        import jax, jax.numpy as jnp
        import numpy as np
        EPS = 1e-12

        def l2_normalize_rows(x):
            nrm = jnp.sqrt(jnp.sum(x * x, axis=1, keepdims=True))
            return x / jnp.maximum(nrm, EPS)
        key = jax.random.key(seed)
        k1, k2, k3, k4 = jax.random.split(key, 4)
        n, din, dout, E = (12500, 256, 256, 200000)
        x = jax.random.normal(k1, (n, din), dtype=jnp.float32)
        edge_index = jax.random.randint(k2, (2, E), 0, n, dtype=jnp.int64)
        s = float(np.sqrt(6.0 / (din + dout)))
        W_gcn = jax.random.uniform(k3, (din, dout), jnp.float32, -s, s)
        b_gcn = jnp.zeros((dout,), jnp.float32)
        W_V = jax.random.uniform(k4, (din, dout), jnp.float32, -s, s)
        return {'x': x, 'edge_index': edge_index, 'W_gcn': W_gcn, 'b_gcn': b_gcn, 'W_V': W_V}
    _L0_gnn_all = _L0_gnn_setup()
    _L0_gnn_in = {k: v for k, v in _L0_gnn_all.items() if k in ('W_gcn', 'b_gcn', 'W_V')}
    del _L0_gnn_all

    def _L0_mix_setup():
        import jax, jax.numpy as jnp
        import numpy as np
        HEADS, DIM_HEAD = (8, 64)
        EPS = 1e-05

        def instance_norm(t):
            mu = jnp.mean(t, axis=-1, keepdims=True)
            var = jnp.mean((t - mu) ** 2, axis=-1, keepdims=True)
            return (t - mu) * jax.lax.rsqrt(var + EPS)
        key = jax.random.key(seed)
        k1, k2, k3, k4 = jax.random.split(key, 4)
        B, N, D = (8, 1024, 256)
        inner = HEADS * DIM_HEAD
        x = jax.random.normal(k1, (B, N, D), jnp.float32)
        w_qkv = jax.random.normal(k2, (3 * inner, D), jnp.float32) / np.sqrt(D).astype(np.float32)
        w_out = jax.random.normal(k3, (D, inner), jnp.float32) / np.sqrt(inner).astype(np.float32)
        b_out = 0.01 * jax.random.normal(k4, (D,), jnp.float32)
        return {'x': x, 'w_qkv': w_qkv, 'w_out': w_out, 'b_out': b_out}
    _L0_mix_all = _L0_mix_setup()
    _L0_mix_in = {k: v for k, v in _L0_mix_all.items() if k in ('w_qkv', 'w_out', 'b_out')}
    del _L0_mix_all

    def _L0_ffn_setup():
        import jax, jax.numpy as jnp
        import numpy as np
        B, A = (512, 8)
        IN, OUT = (256, 256)
        SH1, SH2 = (256, 128)
        EH1, EH2 = (128, 64)
        E, TOPK = (4, 2)

        def _shared_mlp(x, W1, b1, W2, b2, W3, b3):
            h = jax.nn.relu(x @ W1 + b1)
            h = jax.nn.relu(h @ W2 + b2)
            return h @ W3 + b3

        def _experts_mlp(x, eW1, eb1, eW2, eb2, eW3, eb3):
            h = jax.nn.relu(jnp.einsum('baf,efh->ebah', x, eW1) + eb1[:, None, None, :])
            h = jax.nn.relu(jnp.einsum('ebah,ehg->ebag', h, eW2) + eb2[:, None, None, :])
            o = jnp.einsum('ebag,ego->ebao', h, eW3) + eb3[:, None, None, :]
            return jnp.moveaxis(o, 0, -1)
        key = jax.random.key(seed)
        ks = jax.random.split(key, 16)
        s = 0.05
        return {'x': jax.random.normal(ks[0], (B, A, IN), jnp.float32), 'sW1': jax.random.normal(ks[1], (IN, SH1), jnp.float32) * s, 'sb1': jnp.zeros((SH1,), jnp.float32), 'sW2': jax.random.normal(ks[2], (SH1, SH2), jnp.float32) * s, 'sb2': jnp.zeros((SH2,), jnp.float32), 'sW3': jax.random.normal(ks[3], (SH2, OUT), jnp.float32) * s, 'sb3': jnp.zeros((OUT,), jnp.float32), 'eW1': jax.random.normal(ks[4], (E, IN, EH1), jnp.float32) * s, 'eb1': jnp.zeros((E, EH1), jnp.float32), 'eW2': jax.random.normal(ks[5], (E, EH1, EH2), jnp.float32) * s, 'eb2': jnp.zeros((E, EH2), jnp.float32), 'eW3': jax.random.normal(ks[6], (E, EH2, OUT), jnp.float32) * s, 'eb3': jnp.zeros((E, OUT), jnp.float32), 'gW': jax.random.normal(ks[7], (IN, E), jnp.float32) * s, 'gb': jnp.zeros((E,), jnp.float32)}
    _L0_ffn_all = _L0_ffn_setup()
    _L0_ffn_in = {k: v for k, v in _L0_ffn_all.items() if k in ('sW1', 'sb1', 'sW2', 'sb2', 'sW3', 'sb3', 'eW1', 'eb1', 'eW2', 'eb2', 'eW3', 'eb3', 'gW', 'gb')}
    del _L0_ffn_all
    return {'x': x, 'src': src, 'dst': dst, 'L0_gnn_W_gcn': _L0_gnn_in['W_gcn'], 'L0_gnn_b_gcn': _L0_gnn_in['b_gcn'], 'L0_gnn_W_V': _L0_gnn_in['W_V'], 'L0_mix_w_qkv': _L0_mix_in['w_qkv'], 'L0_mix_w_out': _L0_mix_in['w_out'], 'L0_mix_b_out': _L0_mix_in['b_out'], 'L0_ffn_sW1': _L0_ffn_in['sW1'], 'L0_ffn_sb1': _L0_ffn_in['sb1'], 'L0_ffn_sW2': _L0_ffn_in['sW2'], 'L0_ffn_sb2': _L0_ffn_in['sb2'], 'L0_ffn_sW3': _L0_ffn_in['sW3'], 'L0_ffn_sb3': _L0_ffn_in['sb3'], 'L0_ffn_eW1': _L0_ffn_in['eW1'], 'L0_ffn_eb1': _L0_ffn_in['eb1'], 'L0_ffn_eW2': _L0_ffn_in['eW2'], 'L0_ffn_eb2': _L0_ffn_in['eb2'], 'L0_ffn_eW3': _L0_ffn_in['eW3'], 'L0_ffn_eb3': _L0_ffn_in['eb3'], 'L0_ffn_gW': _L0_ffn_in['gW'], 'L0_ffn_gb': _L0_ffn_in['gb']}

def reference(x, src, dst, L0_gnn_W_gcn, L0_gnn_b_gcn, L0_gnn_W_V, L0_mix_w_qkv, L0_mix_w_out, L0_mix_b_out, L0_ffn_sW1, L0_ffn_sb1, L0_ffn_sW2, L0_ffn_sb2, L0_ffn_sW3, L0_ffn_sb3, L0_ffn_eW1, L0_ffn_eb1, L0_ffn_eW2, L0_ffn_eb2, L0_ffn_eW3, L0_ffn_eb3, L0_ffn_gW, L0_ffn_gb):
    import jax
    import jax.numpy as jnp

    def _L0_gnn_ref(x, edge_index, W_gcn, b_gcn, W_V):
        import jax, jax.numpy as jnp
        import numpy as np
        EPS = 1e-12

        def l2_normalize_rows(x):
            nrm = jnp.sqrt(jnp.sum(x * x, axis=1, keepdims=True))
            return x / jnp.maximum(nrm, EPS)
        n = x.shape[0]
        beta = 0.1
        H = l2_normalize_rows(x)
        XW = H @ W_gcn
        loop = jnp.arange(n, dtype=edge_index.dtype)
        src = jnp.concatenate([edge_index[0], loop])
        dst = jnp.concatenate([edge_index[1], loop])
        deg = jax.ops.segment_sum(jnp.ones_like(dst, dtype=XW.dtype), dst, num_segments=n)
        dinv = jax.lax.rsqrt(jnp.maximum(deg, 1e-30))
        norm = dinv[src] * dinv[dst]
        msg = XW[src] * norm[:, None]
        z_local = jax.ops.segment_sum(msg, dst, num_segments=n) + b_gcn
        HtH = H.T @ H
        z_global = beta / n * (H @ HtH @ W_V)
        out = jax.nn.relu(z_local + z_global)
        return l2_normalize_rows(out)

    def _L0_mix_ref(x, w_qkv, w_out, b_out):
        import jax, jax.numpy as jnp
        import numpy as np
        HEADS, DIM_HEAD = (8, 64)
        EPS = 1e-05

        def instance_norm(t):
            mu = jnp.mean(t, axis=-1, keepdims=True)
            var = jnp.mean((t - mu) ** 2, axis=-1, keepdims=True)
            return (t - mu) * jax.lax.rsqrt(var + EPS)
        B, N, _ = x.shape
        H, Dh = (HEADS, DIM_HEAD)
        qkv = jnp.einsum('bnd,ed->bne', x, w_qkv)
        q, k, v = jnp.split(qkv, 3, axis=-1)

        def to_heads(t):
            return t.reshape(B, N, H, Dh).transpose(0, 2, 1, 3)
        q, k, v = (to_heads(q), to_heads(k), to_heads(v))
        k = instance_norm(k)
        v = instance_norm(v)
        dots = jnp.einsum('bhnd,bhne->bhde', k, v)
        out = jnp.einsum('bhnd,bhde->bhne', q, dots) / N
        out = out.transpose(0, 2, 1, 3).reshape(B, N, H * Dh)
        return jnp.einsum('bne,de->bnd', out, w_out) + b_out

    def _L0_ffn_ref(x, sW1, sb1, sW2, sb2, sW3, sb3, eW1, eb1, eW2, eb2, eW3, eb3, gW, gb):
        import jax, jax.numpy as jnp
        import numpy as np
        B, A = (512, 8)
        IN, OUT = (256, 256)
        SH1, SH2 = (256, 128)
        EH1, EH2 = (128, 64)
        E, TOPK = (4, 2)

        def _shared_mlp(x, W1, b1, W2, b2, W3, b3):
            h = jax.nn.relu(x @ W1 + b1)
            h = jax.nn.relu(h @ W2 + b2)
            return h @ W3 + b3

        def _experts_mlp(x, eW1, eb1, eW2, eb2, eW3, eb3):
            h = jax.nn.relu(jnp.einsum('baf,efh->ebah', x, eW1) + eb1[:, None, None, :])
            h = jax.nn.relu(jnp.einsum('ebah,ehg->ebag', h, eW2) + eb2[:, None, None, :])
            o = jnp.einsum('ebag,ego->ebao', h, eW3) + eb3[:, None, None, :]
            return jnp.moveaxis(o, 0, -1)
        all_out = _experts_mlp(x, eW1, eb1, eW2, eb2, eW3, eb3)
        shared = _shared_mlp(x, sW1, sb1, sW2, sb2, sW3, sb3)
        gates = jax.nn.softmax(x @ gW + gb, axis=-1)
        topv, topi = jax.lax.top_k(gates, TOPK)
        topw = jax.nn.softmax(topv, axis=-1)
        sel = jnp.take_along_axis(all_out, topi[:, :, None, :], axis=-1)
        gated = jnp.sum(sel * topw[:, :, None, :], axis=-1)
        return shared + gated
    edge_index = jnp.stack([src, dst])
    xn = _layernorm(x, axis=-1)
    x = x + _L0_gnn_ref(xn, edge_index, L0_gnn_W_gcn, L0_gnn_b_gcn, L0_gnn_W_V) + _L0_mix_ref(xn[None], L0_mix_w_qkv, L0_mix_w_out, L0_mix_b_out)[0]
    x = x + _L0_ffn_ref(_layernorm(x, axis=-1)[None], L0_ffn_sW1, L0_ffn_sb1, L0_ffn_sW2, L0_ffn_sb2, L0_ffn_sW3, L0_ffn_sb3, L0_ffn_eW1, L0_ffn_eb1, L0_ffn_eW2, L0_ffn_eb2, L0_ffn_eW3, L0_ffn_eb3, L0_ffn_gW, L0_ffn_gb)[0]
    return x

_drawn_inputs = setup_inputs


def setup_inputs(seed=0):
    import zlib

    import numpy as np

    out = dict(_drawn_inputs(seed))
    spreads = {'L0_gnn_b_gcn': (0.0, 0.1),
     'L0_ffn_sb1': (0.0, 0.451),
     'L0_ffn_sb2': (0.0, 0.1),
     'L0_ffn_sb3': (0.0, 0.1),
     'L0_ffn_eb1': (0.0, 0.8),
     'L0_ffn_eb2': (0.0, 0.539),
     'L0_ffn_eb3': (0.0, 0.1),
     'L0_ffn_gb': (0.0, 0.391)}
    factors = {'L0_gnn_W_gcn': 6.167, 'L0_gnn_W_V': 8.0, 'L0_mix_b_out': 6.32}
    for name, (base, spread) in spreads.items():
        noise = np.random.default_rng([zlib.crc32(name.encode()), seed]).standard_normal(out[name].shape)
        drawn = base * np.exp(spread * noise) if base else spread * noise
        out[name] = jnp.asarray(drawn.astype(out[name].dtype))
    for name, factor in factors.items():
        out[name] = (out[name] * factor).astype(out[name].dtype)
    return out
```

```python
import math
from contextlib import ExitStack

import concourse.bass as bass
import numpy as np
from concourse import mybir
from concourse.bass import ds

F32, BF16, I32 = mybir.dt.float32, mybir.dt.bfloat16, mybir.dt.int32
ALU = mybir.AluOpType
ACT = mybir.ActivationFunctionType
AX = mybir.AxisListType.X

N, E = 12500, 212500
P = 128
NT = -(-N // P)
NPAD = NT * P
LAST = N - (NT - 1) * P
D = 256
K = 7
GE = K * P
NG = E // GE
TAILT = -(-(E - NG * GE) // P)
ET = NG * K + TAILT
W = 64
ZN = NPAD + W
HEADS, DH = 8, 64
INNER = HEADS * DH
NP = NT // 2
CH = 7
NCH = NT // CH
GP1 = NT
GPP = 3
NPL = (NG - GP1) // GPP
EPS_LN = 1e-5
EPS_NRM = 1e-12
BETA = 0.1
NWEIGHTS = 17


def wait(e, sem, value):
    if isinstance(value, int) and value <= 0:
        return
    e.wait_ge(sem, value)


def build(nc, x, src_t, dst_t, dst_rows, w_kvT, w_q, w_oT, w_V, w_gcn, b_gcn, b_out, sW1, eW1, sW2, eW2,
          sW3, eW3, gW, gb, h_bias, o_bias, c_ident, c_iota, c_rank, c_limit, c_pick, c_low, c_trash, out):
    table = nc.dram_tensor("table", (NPAD, 3 * D), BF16, kind="Internal").ap()
    zsum = nc.dram_tensor("zsum", (NPAD + P, D), F32, kind="Internal").ap()
    ctx = ExitStack()
    with ctx:
        def sb(name, shape, dt=F32):
            return ctx.enter_context(nc.sbuf_tensor(name, shape, dt))

        def sem(name):
            return ctx.enter_context(nc.semaphore(name))

        zT = sb("zT", [P, 2, ZN])
        G = sb("G", [P, 2 * K, 3 * D], BF16)
        idx = sb("idx", [P, 2, K], I32)
        oh = sb("oh", [P, 2, K, W], BF16)
        dloc = sb("dloc", [P, ET], BF16)
        base_i = sb("base_i", [1, NG + 1], I32)
        flag_i = sb("flag_i", [1, 1], I32)
        ident = sb("ident", [P, P])
        iota = sb("iota", [P, P])
        iota_w = sb("iota_w", [P, W], BF16)
        ones = sb("ones", [P, P])
        ones_b = sb("ones_b", [P, 1], BF16)
        rank = sb("rank", [P, 8])
        bB = sb("bB", [P, D])
        boB = sb("boB", [P, D])
        gbB = sb("gbB", [P, 8])
        hb = sb("hb", [P, 9])
        ob = sb("ob", [5, D])
        pick = sb("pick", [5, 2, P])
        wkv = sb("wkv", [P, 2, 2 * INNER])
        wg = sb("wg", [P, 2, D])
        mp = sb("mp", [P, 2, 2 * D])
        w1 = sb("w1", [P, 2, 6, P])
        w2s = sb("w2s", [P, 2, P])
        w2e = sb("w2e", [P, 4, 64])
        w3 = sb("w3", [P, 3, D])
        gw = sb("gw", [P, 2, 4])
        deg, dsq, c_, cb, cD, cbD, q, q2, q264, tiny2 = (
            sb(n, [P, NT]) for n in ("deg", "dsq", "c", "cb", "cD", "cbD", "q", "q2", "q264", "tiny2"))
        stat = sb("stat", [P, NT, 2])
        lnb = sb("lnb", [P, 1])
        bns = sb("bns", [P, CH, 6])
        bna = sb("bna", [P, CH, 2])

        arena = sb("arena", [P, 9856])
        at = [0]

        def cut(n, *shape):
            v = arena[:, at[0]:at[0] + n]
            at[0] += n
            if len(shape) == 2:
                v = v.rearrange("p (a b) -> p a b", a=shape[0])
            if len(shape) == 3:
                v = v.rearrange("p (a b c) -> p a b c", a=shape[0], b=shape[1])
            return v

        xc = cut(2 * CH * D, 2, CH, D)
        tc = cut(2 * CH * D, 2, CH, D)
        tb = G[:, :, :].rearrange("p (s k) f -> p s k f", s=2)
        at[0] = 0
        xk, tk, dk = cut(512, 2, D), cut(512, 2, D), cut(512, 2, D)
        ttk = cut(512, 2, 2, P)
        sq = cut(1024, 16, DH)
        ks, vs = cut(1024, 2, INNER), cut(1024, 2, INNER)
        msum, mm, pr, al, al2, kr, kn = cut(16), cut(16), cut(8), cut(8), cut(8), cut(8), cut(8)
        wq_m, wo_m, r_m = cut(1024, 4, D), cut(1024, 4, D), cut(1024, 4, D)
        hh, wv_m = cut(512, 2, D), cut(512, 2, D)
        bd = cut(512, 4, P)
        assert at[0] <= 9856
        at[0] = 0
        xf = cut(1024, 4, D)
        tf, ttf, ag = cut(512, 2, D), cut(512, 2, 2 * P), cut(512, 2, 2 * P)
        vv, rr = cut(512, 2, D), cut(512, 2, D)
        sqf = cut(256)
        yy = cut(1024, 2, 2, D)
        uu = cut(512, 2, D)
        uT = cut(512, 2, 2 * P)
        h1 = cut(1536, 6, 2 * P)
        h2 = cut(768, 3, 2 * P)
        oo = cut(1024, 2, 2, D)
        wT = cut(256)
        lg, e_g, gt, o1, g2, o2, t8 = (cut(8, 2, 4) for _ in range(7))
        w5 = cut(10, 2, 5)
        v2 = [cut(2) for _ in range(12)]
        ss, lo, rs0, nt_, inv, vr, rs1, rstd, nb_ = (cut(2) for _ in range(9))
        bnf = cut(12, 2, 6)
        mvf = cut(4, 2, 2)
        assert at[0] <= 9856

        zflat = zT[:, :, :].rearrange("p c n -> p (c n)")
        dst_i = zflat[:, 0:ET].bitcast(I32)
        dst_f = zflat[:, ET:2 * ET]
        o = 2 * ET
        deg_row = zflat[0:1, o:o + ZN]
        deg_98 = zflat[0:NT, o + ZN + 1024:o + ZN + 1024 + P]
        base_f = zflat[0:1, o + ZN:o + ZN + NG + 1]
        lim = zflat[0:1, o + ZN + 256:o + ZN + 256 + NG + 1]
        o = o + ZN + 512
        mx = zflat[:, o:o + 8]
        wmean = zflat[:, o + 8:o + 40]
        t98 = zflat[:, o + 64:o + 64 + NT]
        pb = [ctx.enter_context(nc.psum_tensor(f"bank{i}", [P, 512], F32)) for i in range(8)]
        AGG = [pb[s][:, 0:2 * W].rearrange("p (c w) -> p c w", c=2) for s in range(2)]

        S = {n: sem("s_" + n) for n in (
            "iota_w deg_c colg const weights dst xin0 xin1 xin_last xpad xuse base_f base_b range_v range_t flag flag_c "
            "deg_zero deg_oh deg_ps deg_add deg_row deg_98 deg_t cols cols_c consts_made wcent "
            "bn bna t_done t_raw t_hi t_r1 t_mid t_lo t_out0 t_out1 zclear zero_l psum0 "
            "idx0 idx1 gat0 gat1 oh agg acc "
            "kn xk0 xk1 xkpad td tr tt k_ps v_ps sq vs chain_kv ks dots hth mid_w mid_p mid_d "
            "rs stand_v stand_p stand_s xf0 xf1 xf2 xf3 xfpad tf ttr ttf ag p12 vv ssq rr y st nb u tru ut gates lg eg gap ed w5 wt wtc "
            "h1 h1e wb h2 h2e h2w pout oo st0 st1 "
            "g_idx g_gat g_e g_ch g_sum g_copy g_sc g_zero g_clear g_ztr g_zld g_zcp g_oh g_ab g_dps").split()}

        def stand(e):
            e.sem_inc(S[{"Pool": "stand_p", "SP": "stand_s"}.get(e.engine.name, "stand_v")], 1)

        def sp_group_idx(sp, g, it, s, k=K):
            wait(sp, S[f"gat{s}"], it * (16 * K))
            stand(sp)
            sp.dma_start(idx[:, s, 0:k], src_t[:, ds(g * K, k)]).then_inc(S[f"idx{s}"], 16)

        def pool_group(pool, g, it, s, k=K):
            pool.wait_ge(S[f"idx{s}"], it * 16 + 16)
            wait(pool, S["agg"], g - 1)
            stand(pool)
            for j in range(k):
                pool.indirect_dma_start(G[:, s * K + j, :], None, table,
                                        bass.IndirectOffsetOnAxis(ap=idx[:, s, j:j + 1], axis=0)
                                        ).then_inc(S[f"gat{s}"], 16)

        def dve_onehot(dve, g, s, k=K):
            wait(dve, S["agg"], g - 1)
            nc.vector.tensor_tensor(oh[:, s, 0:k, :],
                                    dloc[:, ds(g * K, k)].unsqueeze(2).to_broadcast([P, k, W]),
                                    iota_w[:, :].unsqueeze(1).to_broadcast([P, k, W]),
                                    ALU.is_equal).then_inc(S["oh"], 1)

        def pe_group(pe, g, it, s, k=K):
            pe.wait_ge(S[f"gat{s}"], it * (16 * K) + 16 * k)
            pe.wait_ge(S["oh"], g + 1)
            wait(pe, S["acc"], g - 1)
            for j in range(k):
                for part in range(3):
                    for c in range(2):
                        o_ = part * D + c * P
                        last = nc.tensor.matmul(AGG[s][:, c, :], G[:, s * K + j, o_:o_ + P], oh[:, s, j, :],
                                                start=(j == 0 and part == 0 and c == 0),
                                                stop=(j == k - 1 and part == 2 and c == 1),
                                                skip_group_check=True)
            last.then_inc(S["agg"], 1)

        def dve_group_add(dve, g, s):
            dve.wait_ge(S["agg"], g + 1)
            wait(dve, S["acc"], g)
            b = dve.value_load(base_i[0:1, ds(g, 1)], min_val=0, max_val=NPAD)
            win = zT[:, :, ds(b, W)]
            nc.vector.tensor_tensor(win, win, AGG[s], ALU.add).then_inc(S["acc"], 1)

        def dve_polish(dve, v, guess, tmp, to, sem_, at_):
            V = nc.vector
            V.scalar_tensor_tensor(tmp, guess, -0.5, guess, ALU.mult, ALU.mult).then_inc(sem_, 1)
            dve.wait_ge(sem_, at_ + 1)
            V.tensor_tensor(tmp, tmp, v, ALU.mult).then_inc(sem_, 1)
            dve.wait_ge(sem_, at_ + 2)
            V.scalar_tensor_tensor(to, tmp, 1.5, guess, ALU.add, ALU.mult).then_inc(sem_, 1)
            dve.wait_ge(sem_, at_ + 3)

        def sp_kv_x(sp, i, s, last=False):
            wait(sp, S["td"], 2 * i - 2)
            stand(sp)
            if last:
                sp.wait_ge(S["xkpad"], 1)
            rows = LAST if last else P
            sp.dma_start(xk[0:rows, s, :], x[ds(i * P, rows), :]).then_inc(S[f"xk{s}"], 16)

        def act_kv_scale(act, i, it, s):
            act.wait_ge(S[f"xk{s}"], it * 16 + 16)
            wait(act, S["hth"], i - 1)
            nc.scalar.activation(tk[:, s, :], xk[:, s, :], ACT.Identity, scale=c_[:, ds(i, 1)],
                                 bias=cb[:, ds(i, 1)]).then_inc(S["td"], 1)
            nc.scalar.activation(dk[:, s, :], xk[:, s, :], ACT.Identity, scale=cD[:, ds(i, 1)],
                                 bias=cbD[:, ds(i, 1)]).then_inc(S["td"], 1)

        def pe_kv_transpose(pe, i, s):
            pe.wait_ge(S["td"], 2 * i + 2)
            wait(pe, S["tt"], i)
            for c in range(2):
                last = nc.tensor.transpose(pb[6][:, c * P:c * P + P],
                                           tk[:, s, c * P:c * P + P], ident[:, :])
            last.then_inc(S["tr"], 1)

        def act_kv_transposed(act, i, s):
            act.wait_ge(S["tr"], i + 1)
            wait(act, S["v_ps"], i - 1)
            nc.scalar.activation(ttk[:, s, :, :], pb[6][:, 0:256].rearrange(
                "p (c n) -> p c n", c=2), ACT.Copy).then_inc(S["tt"], 1)

        def pe_kv(pe, i, s):
            pe.wait_ge(S["tt"], i + 1)
            wait(pe, S["ks"], i)
            wait(pe, S["sq"], 2 * i)
            for half, bank, signal in ((0, 2, "k_ps"), (1, 3, "v_ps")):
                if half:
                    wait(pe, S["vs"], i)
                for c in range(2):
                    last = nc.tensor.matmul(pb[bank][:, :], ttk[:, s, c, :],
                                            wkv[:, c, half * INNER:(half + 1) * INNER],
                                            start=(c == 0), stop=(c == 1))
                last.then_inc(S[signal], 1)

        def act_kv(act, i, s):
            act.wait_ge(S["k_ps"], i + 1)
            wait(act, S["chain_kv"], 7 * i - 6)
            nc.scalar.activation(sq[:, 0:8, :].rearrange("p h d -> p (h d)"), pb[2][:, :],
                                 ACT.Square).then_inc(S["sq"], 1)
            act.wait_ge(S["v_ps"], i + 1)
            nc.scalar.activation(sq[:, 8:16, :].rearrange("p h d -> p (h d)"), pb[3][:, :],
                                 ACT.Square).then_inc(S["sq"], 1)
            wait(act, S["dots"], i - 1)
            nc.scalar.activation(vs[:, s, :], pb[3][:, :], ACT.Copy).then_inc(S["vs"], 1)
            act.wait_ge(S["chain_kv"], 7 * i + 3)
            nc.scalar.activation(kn, pr, ACT.Ln).then_inc(S["kn"], 1)
            act.wait_ge(S["kn"], 2 * i + 1)
            nc.scalar.activation(kr, kn, ACT.Exp, scale=-0.5).then_inc(S["kn"], 1)

        def dve_kv(dve, i, s):
            dve.wait_ge(S["sq"], 2 * i + 2)
            ch = S["chain_kv"]
            nc.vector.tensor_reduce(msum, sq, AX, ALU.add).then_inc(ch, 1)
            dve.wait_ge(ch, 7 * i + 1)
            nc.vector.tensor_scalar(mm, msum, q264[:, ds(i, 1)], EPS_LN, ALU.mult, ALU.add).then_inc(ch, 1)
            dve.wait_ge(ch, 7 * i + 2)
            nc.vector.tensor_tensor(pr, mm[:, 0:8], mm[:, 8:16], ALU.mult).then_inc(ch, 1)
            dve.wait_ge(S["kn"], 2 * i + 2)
            dve_polish(dve, pr, kr, al, al2, ch, 7 * i + 3)
            nc.vector.tensor_scalar(al, al2, q2[:, ds(i, 1)], None, ALU.mult).then_inc(ch, 1)
            dve.wait_ge(ch, 7 * i + 7)
            wait(dve, S["dots"], i - 1)
            nc.vector.tensor_tensor(ks[:, s, :].rearrange("p (h d) -> p h d", h=HEADS),
                                    pb[2][:, :].rearrange("p (h d) -> p h d", h=HEADS),
                                    al.unsqueeze(2).to_broadcast([P, HEADS, DH]),
                                    ALU.mult).then_inc(S["ks"], 1)

        def pe_dots(pe, i, s):
            pe.wait_ge(S["ks"], i + 1)
            pe.wait_ge(S["vs"], i + 1)
            for h in range(4):
                last = nc.tensor.matmul(pb[4][:, h * P:h * P + P], vs[:, s, h * P:h * P + P],
                                        ks[:, s, h * P:h * P + P], start=False, stop=False,
                                        skip_group_check=True)
            last.then_inc(S["dots"], 1)

        def pe_hth(pe, i, s):
            nc.tensor.matmul(pb[5][:, 0:256], tk[:, s, 0:P], dk[:, s, :], start=False, stop=False,
                             skip_group_check=True)
            nc.tensor.matmul(pb[5][:, 256:384], tk[:, s, P:D], dk[:, s, P:D], start=False, stop=False,
                             skip_group_check=True).then_inc(S["hth"], 1)

        def sp_mid(sp):
            sp.dma_start(wv_m, w_V.rearrange("(c p) n -> p c n", p=P)).then_inc(S["mid_w"], 16)
            sp.dma_start(wq_m, w_q.rearrange("(h p) n -> p h n", p=P)).then_inc(S["mid_w"], 16)
            sp.dma_start(wo_m, w_oT.rearrange("(h p) n -> p h n", p=P)).then_inc(S["mid_w"], 16)

        def dve_mid(dve):
            mid = S["mid_d"]
            dve.wait_ge(S["hth"], NT)
            dve.wait_ge(S["dots"], NT)
            nc.vector.tensor_copy(hh[:, 0, :], pb[5][:, 0:256]).then_inc(mid, 1)
            nc.vector.tensor_copy(hh[:, 1, P:D], pb[5][:, 256:384]).then_inc(mid, 1)
            nc.vector.memset(bd, 0.0).then_inc(mid, 1)
            dve.wait_ge(mid, 3)
            for h in range(2):
                o_ = h * DH
                nc.vector.tensor_copy(bd[o_:o_ + DH, :, o_:o_ + DH], pb[4][o_:o_ + DH, :].rearrange(
                    "p (h d) -> p h d", h=4)[:, :, o_:o_ + DH]).then_inc(mid, 1)
            dve.wait_ge(S["mid_p"], 1)
            nc.vector.tensor_copy(hh[:, 1, 0:P], pb[7][:, 0:P]).then_inc(mid, 1)
            dve.wait_ge(S["mid_p"], 2)
            for b in range(2):
                nc.vector.tensor_copy(r_m[:, 2 * b:2 * b + 2, :], pb[2 + b][:, :].rearrange(
                    "p (h n) -> p h n", h=2)).then_inc(mid, 1)
            dve.wait_ge(S["mid_p"], 3)
            nc.vector.tensor_scalar(mp[:, :, 0:D], pb[6][:, :].rearrange("p (c n) -> p c n", c=2),
                                    BETA / N, None, ALU.mult).then_inc(mid, 1)
            dve.wait_ge(S["mid_p"], 4)
            nc.vector.tensor_scalar(mp[:, :, D:2 * D], pb[7][:, :].rearrange("p (c n) -> p c n", c=2),
                                    1.0 / N, None, ALU.mult).then_inc(mid, 1)
            nc.vector.memset(w5, 1.0).then_inc(mid, 1)
            dve.wait_ge(mid, 11)

        def pe_mid(pe):
            pe.wait_ge(S["mid_w"], 48)
            pe.wait_ge(S["mid_d"], 5)
            nc.tensor.transpose(pb[7][:, 0:P], hh[:, 0, P:D], ident[:, :]).then_inc(S["mid_p"], 1)
            for h in range(4):
                last = nc.tensor.matmul(pb[2 + h // 2][:, (h % 2) * D:(h % 2) * D + D], bd[:, h, :],
                                        wo_m[:, h, :], start=True, stop=True)
            last.then_inc(S["mid_p"], 1)
            pe.wait_ge(S["mid_d"], 6)
            for m in range(2):
                for c in range(2):
                    last = nc.tensor.matmul(pb[6][:, m * D:m * D + D], hh[:, c, m * P:m * P + P],
                                            wv_m[:, c, :], start=(c == 0), stop=(c == 1))
            last.then_inc(S["mid_p"], 1)
            pe.wait_ge(S["mid_d"], 8)
            for m in range(2):
                for h in range(4):
                    last = nc.tensor.matmul(pb[7][:, m * D:m * D + D], wq_m[:, h, m * P:m * P + P],
                                            r_m[:, h, :], start=(h == 0), stop=(h == 3))
            last.then_inc(S["mid_p"], 1)
            pe.wait_ge(S["mid_d"], 11)

        def sp_a(sp, j, s, last=False):
            for t in range(2):
                wait(sp, S["y"], 6 * j - 6)
                stand(sp)
                full = not (last and t == 1)
                if not full:
                    sp.wait_ge(S["xfpad"], 1)
                rows = P if full else LAST
                sp.dma_start(xf[0:rows, 2 * s + t, :], x[ds((2 * j + t) * P, rows), :]).then_inc(
                    S[f"xf{2 * s + t}"], 16)

        def act_a_scale(act, j, it, s):
            wait(act, S["ttr"], 2 * j)
            for t in range(2):
                act.wait_ge(S[f"xf{2 * s + t}"], it * 16 + 16)
                nc.scalar.activation(tf[:, t, :], xf[:, 2 * s + t, :], ACT.Identity,
                                     scale=c_[:, ds(2 * j + t, 1)],
                                     bias=cb[:, ds(2 * j + t, 1)]).then_inc(S["tf"], 1)

        def pe_a_transpose(pe, j):
            for t in range(2):
                pe.wait_ge(S["tf"], 2 * j + t + 1)
                wait(pe, S["vv"], 4 * j)
                for c in range(2):
                    last = nc.tensor.transpose(pb[2][:, t * 256 + c * P:t * 256 + c * P + P],
                                               tf[:, t, c * P:c * P + P], ident[:, :])
                last.then_inc(S["ttr"], 1)

        def act_a_transposed(act, j):
            wait(act, S["p12"], 2 * j)
            for t in range(2):
                act.wait_ge(S["ttr"], 2 * j + 2)
                nc.scalar.activation(ttf[:, t, :], pb[2][:, t * 256:t * 256 + 256],
                                     ACT.Copy).then_inc(S["ttf"], 1)

        def dve_a_sum(dve, j, groups):
            wait(dve, S["p12"], 2 * j)
            if groups is not None:
                wait(dve, S["acc"], groups)
            for t in range(2):
                dve.wait_ge(S["ttf"], 2 * j + t + 1)
                nc.vector.tensor_tensor(ag[:, t, :].rearrange("p (c n) -> p c n", c=2),
                                        ttf[:, t, :].rearrange("p (c n) -> p c n", c=2),
                                        zT[:, :, ds((2 * j + t) * P, P)], ALU.add).then_inc(S["ag"], 1)

        def pe_a(pe, j):
            for t in range(2):
                pe.wait_ge(S["ag"], 2 * j + t + 1)
                pe.wait_ge(S["ttf"], 2 * j + 2)
                wait(pe, S["y"], 6 * j)
                for c in range(2):
                    nc.tensor.matmul(pb[2][:, t * D:t * D + D], ag[:, t, c * P:c * P + P], wg[:, c, :],
                                     start=(c == 0), stop=(c == 1))
                for c in range(2):
                    last = nc.tensor.matmul(pb[3 + t][:, :], ttf[:, t, c * P:c * P + P], mp[:, c, :],
                                            start=(c == 0), stop=(c == 1))
                last.then_inc(S["p12"], 1)

        def dve_a_v(dve, j):
            for t in range(2):
                n = 2 * j + t
                dve.wait_ge(S["p12"], 2 * j + 2)
                wait(dve, S["rr"], 2 * j)
                nc.vector.scalar_tensor_tensor(vv[:, t, :], bB[:, :], dsq[:, ds(n, 1)], pb[2][:, t * D:t * D + D],
                                               ALU.mult, ALU.add).then_inc(S["vv"], 1)
                dve.wait_ge(S["vv"], 2 * n + 1)
                nc.vector.scalar_tensor_tensor(vv[:, t, :], pb[3 + t][:, 0:D], deg[:, ds(n, 1)], vv[:, t, :],
                                               ALU.mult, ALU.add).then_inc(S["vv"], 1)

        def act_a_relu(act, j):
            wait(act, S["y"], 6 * j)
            for t in range(2):
                n = 2 * j + t
                act.wait_ge(S["vv"], 2 * n + 2)
                nc.scalar.activation(rr[:, t, :], vv[:, t, :], ACT.Relu).then_inc(S["rr"], 1)
                act.wait_ge(S["rr"], n + 1)
                wait(act, S["ssq"], n)
                nc.scalar.activation(sqf, rr[:, t, :], ACT.Square,
                                     accum_out=ss[:, t:t + 1]).then_inc(S["ssq"], 1)

        NCOLS = 24
        NST = 12

        def dve_a_y(dve, j, s):
            V, st, y, b0 = nc.vector, S["st"], S["y"], NST * j
            dve.wait_ge(S["ssq"], 2 * j + 2)
            V.tensor_tensor(lo, ss, tiny2[:, ds(j * 2, 2)], ALU.max).then_inc(st, 1)
            wait(dve, S["oo"], 2 * j - 2)
            for t in range(2):
                V.scalar_tensor_tensor(yy[:, s, t, :], pb[3 + t][:, D:2 * D], q[:, ds(2 * j + t, 1)],
                                       xf[:, 2 * s + t, :], ALU.mult, ALU.add).then_inc(y, 1)
            dve.wait_ge(S["rs"], 4 * j + 2)
            dve_polish(dve, lo, rs0, nt_, inv, st, b0 + 1)
            dve.wait_ge(y, 6 * j + 2)
            for t in range(2):
                V.scalar_tensor_tensor(yy[:, s, t, :], rr[:, t, :], inv[:, t:t + 1], yy[:, s, t, :],
                                       ALU.mult, ALU.add).then_inc(y, 1)
            dve.wait_ge(y, 6 * j + 4)
            for t in range(2):
                V.tensor_tensor(yy[:, s, t, :], yy[:, s, t, :], boB[:, :], ALU.add).then_inc(y, 1)
            dve.wait_ge(y, 6 * j + 6)
            for t in range(2):
                V.bn_stats(bnf[:, t, :], yy[:, s, t, :]).then_inc(st, 1)
            dve.wait_ge(st, b0 + 6)
            stand(dve)
            for t in range(2):
                V.bn_aggr(mvf[:, t, :], bnf[:, t, :]).then_inc(st, 1)
            dve.wait_ge(st, b0 + 8)
            V.tensor_scalar(vr, mvf[:, :, 1], EPS_LN, None, ALU.add).then_inc(st, 1)
            dve.wait_ge(S["rs"], 4 * j + 4)
            wait(dve, S["u"], 2 * j)
            dve_polish(dve, vr, rs1, nt_, rstd, st, b0 + 9)
            V.scalar_tensor_tensor(nb_, mvf[:, :, 0], -1.0, rstd, ALU.mult, ALU.mult).then_inc(S["nb"], 1)

        def act_a_norms(act, j):
            act.wait_ge(S["st"], NST * j + 1)
            nc.scalar.activation(rs0, lo, ACT.Ln, scale=2.0 ** 20).then_inc(S["rs"], 1)
            act.wait_ge(S["rs"], 4 * j + 1)
            nc.scalar.activation(rs0, rs0, ACT.Exp, scale=-0.5, bias=lnb[:, :]).then_inc(S["rs"], 1)
            act.wait_ge(S["st"], NST * j + 9)
            nc.scalar.activation(rs1, vr, ACT.Ln).then_inc(S["rs"], 1)
            act.wait_ge(S["rs"], 4 * j + 3)
            nc.scalar.activation(rs1, rs1, ACT.Exp, scale=-0.5).then_inc(S["rs"], 1)

        def act_a_u(act, j, s):
            wait(act, S["tru"], j)
            act.wait_ge(S["nb"], j + 1)
            for t in range(2):
                nc.scalar.activation(uu[:, t, :], yy[:, s, t, :], ACT.Identity, scale=rstd[:, t:t + 1],
                                     bias=nb_[:, t:t + 1]).then_inc(S["u"], 1)

        def pe_b_transpose(pe, j):
            pe.wait_ge(S["u"], 2 * j + 2)
            wait(pe, S["h2w"], 2 * j)
            for t in range(2):
                for c in range(2):
                    last = nc.tensor.transpose(pb[5][:, c * 256 + t * P:c * 256 + t * P + P],
                                               uu[:, t, c * P:c * P + P], ident[:, :])
            last.then_inc(S["tru"], 1)

        def act_b_transposed(act, j):
            act.wait_ge(S["tru"], j + 1)
            wait(act, S["h1"], 6 * j)
            nc.scalar.activation(uT, pb[5][:, :].rearrange("p (c n) -> p c n", c=2),
                                 ACT.Copy).then_inc(S["ut"], 1)

        H1PS = [pb[b][:, h * 256:h * 256 + 256] for b in (6, 7, 6) for h in range(2)]
        H2PS = [pb[7][:, 0:256], pb[7][:, 256:512], pb[6][:, 0:256]]
        WBPS = [pb[5][:, 0:256], pb[5][:, 256:512]]
        OPS = [pb[7][:, 0:256], pb[7][:, 256:512]]
        GPS = pb[5][:, 0:8].rearrange("p (t e) -> p t e", t=2)
        WTPS = pb[5][0:5, 0:256]

        def pe_b_first(pe, j):
            pe.wait_ge(S["ut"], j + 1)
            for t in range(2):
                for c in range(2):
                    last = nc.tensor.matmul(GPS[:, t, :], uT[:, c, t * P:t * P + P], gw[:, c, :],
                                            start=(c == 0), stop=(c == 1))
            last.then_inc(S["gates"], 1)
            wait(pe, S["oo"], 2 * j)
            for m in range(6):
                if m == 4:
                    pe.wait_ge(S["h1e"], 6 * j + 2)
                for c in range(2):
                    last = nc.tensor.matmul(H1PS[m], w1[:, c, m, :], uT[:, c, :],
                                            start=(c == 0), stop=(c == 1))
                last.then_inc(S["h1"], 1)

        def act_b_first(act, j, ms):
            for m in ms:
                act.wait_ge(S["h1"], 6 * j + m // 2 * 2 + 2)
                if m == 0:
                    wait(act, S["h2"], 3 * j)
                nc.scalar.activation(h1[:, m, :], H1PS[m], ACT.Relu, bias=hb[:, m:m + 1]).then_inc(S["h1e"], 1)

        NGATE = 21

        def dve_b_gate1(dve, j):
            ga = S["gap"]
            dve.wait_ge(S["gates"], j + 1)
            nc.vector.tensor_tensor(lg, GPS, gbB[:, :].rearrange("p (t e) -> p t e", t=2),
                                    ALU.add).then_inc(ga, 1)
            dve.wait_ge(ga, NGATE * j + 1)
            nc.vector.tensor_reduce(v2[0], lg, AX, ALU.max).then_inc(ga, 1)
            dve.wait_ge(ga, NGATE * j + 2)
            nc.vector.tensor_tensor(lg, lg, v2[0].unsqueeze(2).to_broadcast([P, 2, 4]),
                                    ALU.subtract).then_inc(ga, 1)

        def act_b_gate1(act, j):
            act.wait_ge(S["gap"], NGATE * j + 3)
            nc.scalar.activation(e_g, lg, ACT.Exp).then_inc(S["eg"], 1)

        def dve_b_gate2(dve, j):
            ga = S["gap"]
            n = [3]

            def chain(ins):
                ins.then_inc(ga, 1)
                n[0] += 1
                dve.wait_ge(ga, NGATE * j + n[0])

            V = nc.vector
            rk = rank[:, :].rearrange("p (t e) -> p t e", t=2)

            def bc(v):
                return v.unsqueeze(2).to_broadcast([P, 2, 4])

            dve.wait_ge(S["eg"], j + 1)
            chain(V.tensor_reduce(v2[1], e_g, AX, ALU.add))
            chain(V.reciprocal(v2[2], v2[1]))
            chain(V.tensor_tensor(gt, e_g, bc(v2[2]), ALU.mult))
            chain(V.tensor_reduce(v2[3], gt, AX, ALU.max))
            chain(V.tensor_tensor(t8, gt, bc(v2[3]), ALU.is_equal))
            chain(V.tensor_tensor(t8, t8, rk, ALU.mult))
            chain(V.tensor_reduce(v2[4], t8, AX, ALU.max))
            chain(V.tensor_tensor(o1, rk, bc(v2[4]), ALU.is_equal))
            chain(V.scalar_tensor_tensor(g2, o1, -4.0, gt, ALU.mult, ALU.add))
            chain(V.tensor_reduce(v2[5], g2, AX, ALU.max))
            V.tensor_tensor(v2[7], v2[5], v2[3], ALU.subtract).then_inc(S["lg"], 1)
            chain(V.tensor_tensor(t8, g2, bc(v2[5]), ALU.is_equal))
            chain(V.tensor_tensor(t8, t8, rk, ALU.mult))
            chain(V.tensor_reduce(v2[6], t8, AX, ALU.max))
            chain(V.tensor_tensor(o2, rk, bc(v2[6]), ALU.is_equal))
            assert n[0] == NGATE - 4

        def act_b_gate2(act, j):
            act.wait_ge(S["lg"], j + 1)
            nc.scalar.activation(v2[8], v2[7], ACT.Exp).then_inc(S["ed"], 1)

        def dve_b_gate3(dve, j):
            ga = S["gap"]
            V = nc.vector

            def bc(v):
                return v.unsqueeze(2).to_broadcast([P, 2, 4])

            dve.wait_ge(S["ed"], j + 1)
            V.tensor_scalar(v2[11], v2[8], 1.0, None, ALU.add).then_inc(ga, 1)
            dve.wait_ge(ga, NGATE * j + NGATE - 3)
            V.reciprocal(v2[9], v2[11]).then_inc(ga, 1)
            dve.wait_ge(ga, NGATE * j + NGATE - 2)
            V.tensor_tensor(o1, o1, bc(v2[9]), ALU.mult).then_inc(ga, 1)
            V.tensor_tensor(v2[10], v2[8], v2[9], ALU.mult).then_inc(ga, 1)
            dve.wait_ge(ga, NGATE * j + NGATE)
            V.tensor_tensor(o2, o2, bc(v2[10]), ALU.mult).then_inc(S["w5"], 1)
            dve.wait_ge(S["w5"], 2 * j + 1)
            wait(dve, S["wt"], j)
            V.tensor_tensor(w5[:, :, 0:4], o1, o2, ALU.add).then_inc(S["w5"], 1)

        def pe_b_weights(pe, j):
            pe.wait_ge(S["w5"], 2 * j + 2)
            for t in range(2):
                last = nc.tensor.transpose(WTPS[:, t * P:t * P + P], w5[:, t, :], ident[:, :])
            last.then_inc(S["wt"], 1)

        def dve_b_weights(dve, j):
            dve.wait_ge(S["wt"], j + 1)
            wait(dve, S["pout"], 2 * j)
            nc.vector.tensor_copy(wT[0:5, :], WTPS).then_inc(S["wtc"], 1)

        def pe_b_second(pe, j):
            pe.wait_ge(S["wtc"], j + 1)
            pe.wait_ge(S["h1e"], 6 * j + 6)
            for r in range(2):
                last = nc.tensor.matmul(WBPS[r], pick[:, r, :], wT[0:5, :], start=True, stop=True)
            last.then_inc(S["wb"], 1)
            for c in range(2):
                last = nc.tensor.matmul(H2PS[0], w2s[:, c, :], h1[:, c, :], start=(c == 0), stop=(c == 1))
            last.then_inc(S["h2"], 1)
            for r in range(2):
                for e in range(2):
                    last = nc.tensor.matmul(H2PS[1 + r][e * 64:e * 64 + 64, :], w2e[:, 2 * r + e, :],
                                            h1[:, 2 + 2 * r + e, :], start=True, stop=True)
                last.then_inc(S["h2"], 1)

        def act_b_second(act, j):
            wait(act, S["pout"], 2 * j)
            for m in range(3):
                act.wait_ge(S["h2"], 3 * j + max(m, 1) + 1)
                nc.scalar.activation(h2[:, m, :], H2PS[m], ACT.Relu, bias=hb[:, 6 + m:7 + m]).then_inc(S["h2e"], 1)

        def dve_b_second(dve, j):
            dve.wait_ge(S["wb"], j + 1)
            for r in range(2):
                dve.wait_ge(S["h2e"], 3 * j + 2 + r)
                nc.vector.tensor_tensor(h2[:, 1 + r, :], h2[:, 1 + r, :], WBPS[r], ALU.mult).then_inc(S["h2w"], 1)

        def pe_b_out(pe, j):
            pe.wait_ge(S["h2e"], 3 * j + 3)
            pe.wait_ge(S["h2w"], 2 * j + 2)
            for t in range(2):
                o_ = t * P
                nc.tensor.matmul(OPS[t], h2[:, 0, o_:o_ + P], w3[:, 0, :], start=True, stop=False)
                nc.tensor.matmul(OPS[t], wT[0:5, o_:o_ + P], ob[:, :], start=False, stop=False)
                for r in range(2):
                    last = nc.tensor.matmul(OPS[t], h2[:, 1 + r, o_:o_ + P], w3[:, 1 + r, :],
                                            start=False, stop=(r == 1))
                last.then_inc(S["pout"], 1)

        def dve_b_out(dve, j, it, s):
            wait(dve, S[f"st{s}"], it * 32)
            for t in range(2):
                dve.wait_ge(S["pout"], 2 * j + 2)
                nc.vector.tensor_tensor(oo[:, s, t, :], yy[:, s, t, :], OPS[t], ALU.add).then_inc(S["oo"], 1)

        def sp_b_out(sp, j, s, last=False):
            for t in range(2):
                sp.wait_ge(S["oo"], 2 * j + t + 1)
                stand(sp)
                rows = LAST if last and t == 1 else P
                sp.dma_start(out[ds((2 * j + t) * P, rows), :], oo[0:rows, s, t, :]).then_inc(S[f"st{s}"], 16)

        g_row_i = arena[:, 5400:5528].bitcast(I32)
        g_row, g_cmp = arena[:, 5528:5656], arena[:, 5656:5784]
        g_eq = arena[:, 5784:5848].bitcast(BF16)
        g_sum, g_z = arena[:, 5848:6104], arena[:, 6104:6360]
        g_dst, g_cnt, g_tgt = arena[:, 6360:6361], arena[:, 6361:6362], arena[:, 6362:6363]
        g_tgt_i = arena[:, 6363:6364].bitcast(I32)
        trash, low = arena[:, 6364:6365], arena[:, 6400:6528]
        free = zflat[:, 18000:18000 + 4 * ET]
        g_hi_i, g_lo_i = free[:, 0:ET].bitcast(I32), free[:, ET:2 * ET].bitcast(I32)
        g_hi, g_lo = free[:, 2 * ET:3 * ET], free[:, 3 * ET:4 * ET]
        GD = 11
        g_oha = G[:, 0:4, :].rearrange("p k f -> p (k f)")[:, 0:GD * P].rearrange("p (k n) -> p k n", k=GD)
        g_ohb = G[:, 4:8, :].rearrange("p k f -> p (k f)")[:, 0:GD * P].rearrange("p (k n) -> p k n", k=GD)
        deg_dram = nc.dram_tensor("deg_dram", (1, NPAD), F32, kind="Internal").ap()

        def tiles_in_pairs(engine, step):
            step(0, 0, 0)
            step(1, 0, 1)
            with engine.Fori(1, NP - 1) as it:
                step(it * 2, it, 0)
                step(it * 2 + 1, it, 1)
            step(NT - 2, NP - 1, 0)
            step(NT - 1, NP - 1, 1)

        def pairs_with_groups(engine, step):
            step(0, 0, 0)
            step(1, 0, 1)
            with engine.Fori(1, NPL // 2) as it:
                step(it * 2, it, 0)
                step(it * 2 + 1, it, 1)

        def pairs_alone(engine, step):
            step(0, 0, 0)
            step(1, 0, 1)
            with engine.Fori(1, NP // 2 - 1) as it:
                step(it * 2, it, 0)
                step(it * 2 + 1, it, 1)
            for j in range(NP - 3, NP):
                step(j, j // 2, j % 2)

        def group_at(j, it, s, n):
            return j * GPP + (GP1 + n), it * GPP + (GP1 + GPP * s + n) // 2, (GPP * s + n) % 2

        def choose(engine, fast, general):
            engine.wait_ge(S["flag"], 1)
            f = engine.value_load(flag_i[0:1, 0:1], min_val=0, max_val=1)
            with engine.If(f == 0):
                fast()
            with engine.Else():
                general()

        def constant(i, value):
            return isinstance(i, int) and i == value

        block = ctx.enter_context(nc.Block())

        a_var, a_gd, a_gs, a_gn, a_di, a_sd, a_rn, a_m, a_t = (
            arena[:, 7200 + 100 * k:7200 + 100 * k + NT] for k in range(9))

        @block.sync
        def _(sp):
            sp.dma_start(dst_i, dst_t).then_inc(S["dst"], 16)
            for to, of in ((lim, c_limit), (ident[:, :], c_ident), (iota[:, :], c_iota.to_broadcast([P, P])),
                           (rank[:, :], c_rank.to_broadcast([P, 8]))):
                sp.dma_start(to, of).then_inc(S["const"], 16)

            def load_chunk(c, uses, s):
                wait(sp, S["xuse"], uses - 1)
                stand(sp)
                sp.dma_start(xc[:, s, :, :], x[ds(c * (CH * P), CH * P), :].rearrange(
                    "(k p) d -> p k d", p=P)).then_inc(S[f"xin{s}"], 16)

            def load_last(uses):
                c = NCH - 1
                sp.wait_ge(S["xuse"], uses - 1)
                sp.wait_ge(S["xpad"], 1)
                sp.dma_start(xc[:, 1, 0:CH - 1, :], x[c * CH * P:c * CH * P + (CH - 1) * P, :].rearrange(
                    "(k p) d -> p k d", p=P)).then_inc(S["xin1"], 16)
                sp.dma_start(xc[0:LAST, 1, CH - 1, :], x[(NT - 1) * P:N, :]).then_inc(S["xin_last"], 16)

            load_chunk(0, 0, 0)
            load_chunk(1, 1, 1)
            with sp.Fori(1, NCH // 2 - 1) as it:
                load_chunk(it * 2, it * 2, 0)
                load_chunk(it * 2 + 1, it * 2 + 1, 1)
            load_chunk(NCH - 2, NCH - 2, 0)
            load_last(NCH - 1)
            loads = ((wkv[:, :, :], w_kvT.rearrange("(c p) n -> p c n", p=P)),
                     (wg[:, :, :], w_gcn.rearrange("(c p) n -> p c n", p=P)),
                     (bB[:, :], b_gcn.to_broadcast([P, D])), (boB[:, :], b_out.to_broadcast([P, D])),
                     (gbB[:, 0:4], gb.to_broadcast([P, 4])), (gbB[:, 4:8], gb.to_broadcast([P, 4])),
                     (hb[:, :], h_bias), (ob[:, :], o_bias), (pick[:, :, :], c_pick),
                     (w1[:, :, 0:2, :], sW1.rearrange("(c p) (m n) -> p c m n", p=P, m=2)),
                     (w1[:, 0, 2:6, :], eW1[:, 0:P, :].rearrange("e p n -> p e n")),
                     (w1[:, 1, 2:6, :], eW1[:, P:D, :].rearrange("e p n -> p e n")),
                     (w2s[:, :, :], sW2.rearrange("(c p) n -> p c n", p=P)),
                     (w2e[:, :, :], eW2.rearrange("e p n -> p e n")),
                     (w3[:, 0, :], sW3), (w3[:, 1:3, :], eW3.rearrange("(r p) n -> p r n", p=P)),
                     (gw[:, :, :], gW.rearrange("(c p) n -> p c n", p=P)))
            assert len(loads) == NWEIGHTS
            for to, of in loads:
                sp.dma_start(to, of).then_inc(S["weights"], 16)

            def degrees():
                sp.wait_ge(S["deg_add"], NG + 1)
                sp.dma_start(deg_dram, deg_row[0:1, 0:NPAD]).then_inc(S["deg_row"], 16)
                sp.wait_ge(S["deg_row"], 16)
                sp.dma_start(deg_98, deg_dram.rearrange("o (n p) -> (o n) p", p=P)).then_inc(S["deg_98"], 16)

            choose(sp, degrees, lambda: sp.nop())

            def store_chunk(c, s):
                sp.wait_ge(S["t_lo"], c + 1)
                stand(sp)
                sp.dma_start(table[ds(c * (CH * P), CH * P), :].rearrange("(k p) f -> p k f", p=P),
                             tb[:, s, :, :]).then_inc(S[f"t_out{s}"], 16)

            load_chunk(0, NCH, 0)
            load_chunk(1, NCH + 1, 1)
            with sp.Fori(0, NCH // 2 - 2) as it:
                for s in range(2):
                    load_chunk(it * 2 + (s + 2), it * 2 + (NCH + s + 2), s)
                    store_chunk(it * 2 + s, s)
            load_chunk(NCH - 2, 2 * NCH - 2, 0)
            store_chunk(NCH - 4, 0)
            load_last(2 * NCH - 1)
            store_chunk(NCH - 3, 1)
            store_chunk(NCH - 2, 0)
            store_chunk(NCH - 1, 1)
            sp.wait_ge(S["t_out0"], 16 * (NCH // 2))
            sp.wait_ge(S["t_out1"], 16 * (NCH // 2))
            sp.nop().then_inc(S["t_done"], 1)

            def load_kv(i, s):
                if not constant(i, NT - 2) and not constant(i, NT - 1):
                    sp_kv_x(sp, i + 2, s, constant(i, NT - 3))

            def pairs_end(j):
                sp_b_out(sp, j - 1, (j - 1) % 2)
                if j + 2 < NP:
                    sp_a(sp, j + 2, j % 2, j + 2 == NP - 1)

            def fast():
                for s in range(2):
                    sp_group_idx(sp, s, 0, s)
                    sp_kv_x(sp, s, s)

                def step(i, it, s):
                    load_kv(i, s)
                    sp_group_idx(sp, i + 2, it + 1, s)

                step(0, 0, 0)
                step(1, 0, 1)
                with sp.Fori(1, NP - 2) as it:
                    step(it * 2, it, 0)
                    step(it * 2 + 1, it, 1)
                for i in range(NT - 4, NT):
                    step(i, i // 2, i % 2)
                sp_mid(sp)
                sp.wait_ge(S["mid_d"], 11)
                sp_a(sp, 0, 0)
                sp_a(sp, 1, 1)

                def pair(j, it, s):
                    for n in range(GPP):
                        g, turn, slot = group_at(j, it, s, n)
                        if not (isinstance(j, int) and g + 2 > NG):
                            sp_group_idx(sp, g + 2, turn + 1, slot, TAILT if constant(g, NG - 2) else K)
                    if not constant(j, 0):
                        sp_b_out(sp, j - 1, 1 - s)
                    sp_a(sp, j + 2, s)

                pair(0, 0, 0)
                pair(1, 0, 1)
                with sp.Fori(1, NPL // 2 - 1) as it:
                    pair(it * 2, it, 0)
                    pair(it * 2 + 1, it, 1)
                for j in (NPL - 2, NPL - 1):
                    for n in range(GPP):
                        g = GP1 + j * GPP + n + 2
                        sp_group_idx(sp, g, g // 2, g % 2, K if g < NG else TAILT)
                    sp_b_out(sp, j - 1, (j - 1) % 2)
                    sp_a(sp, j + 2, j % 2)
                for j in range(NPL, NP):
                    pairs_end(j)
                sp_b_out(sp, NP - 1, (NP - 1) % 2, True)

            def general():
                sp.wait_ge(S["g_zero"], 1)
                for c in range(NCH):
                    sp.dma_start(zsum[c * CH * P:(c + 1) * CH * P, :].rearrange("(k p) d -> p k d", p=P),
                                 tc[:, 0, :, :]).then_inc(S["g_clear"], 16)
                sp.dma_start(zsum[NPAD:NPAD + P, :], tc[:, 0, 0, :]).then_inc(S["g_clear"], 16)
                sp.dma_start(low, c_low).then_inc(S["g_clear"], 16)
                sp.dma_start(trash, c_trash).then_inc(S["g_clear"], 16)

                def tile(i):
                    wait(sp, S["g_sc"], i * 16)
                    stand(sp)
                    sp.dma_start(idx[:, 0, 0:1], src_t[:, ds(i, 1)], allow_slow_non_contiguous=True).then_inc(S["g_idx"], 16)
                    sp.dma_start(idx[:, 0, 1:2], dst_t[:, ds(i, 1)], allow_slow_non_contiguous=True).then_inc(S["g_idx"], 16)
                    sp.dma_start(g_row_i, dst_rows[ds(i, 1), :].to_broadcast([P, P])).then_inc(S["g_idx"], 16)

                tile(0)
                with sp.Fori(1, ET) as i:
                    tile(i)
                sp.wait_ge(S["g_sc"], 16 * ET)

                def back(n):
                    wait(sp, S["g_ztr"], n)
                    stand(sp)
                    sp.dma_start(g_z, zsum[ds(n * P, P), :]).then_inc(S["g_zld"], 16)

                back(0)
                with sp.Fori(1, NT) as n:
                    back(n)
                sp.wait_ge(S["g_ztr"], NT)
                for s in range(2):
                    sp_kv_x(sp, s, s)
                load_kv(0, 0)
                load_kv(1, 1)
                with sp.Fori(1, NP - 2) as it:
                    load_kv(it * 2, 0)
                    load_kv(it * 2 + 1, 1)
                for i in range(NT - 4, NT - 2):
                    load_kv(i, i % 2)
                sp_mid(sp)
                sp.wait_ge(S["mid_d"], 11)
                sp_a(sp, 0, 0)
                sp_a(sp, 1, 1)
                sp_a(sp, 2, 0)
                sp_b_out(sp, 0, 0)
                sp_a(sp, 3, 1)
                with sp.Fori(1, NP // 2 - 1) as it:
                    for s in range(2):
                        sp_b_out(sp, it * 2 + (s - 1), 1 - s)
                        sp_a(sp, it * 2 + (s + 2), s)
                for j in range(NP - 3, NP):
                    pairs_end(j)
                sp_b_out(sp, NP - 1, (NP - 1) % 2, True)

            choose(sp, fast, general)
            sp.wait_ge(S["st0"], 32 * (NP - NP // 2))
            sp.wait_ge(S["st1"], 32 * (NP // 2))

        @block.gpsimd
        def _(pool):
            pool.memset(ones[:, :], 1.0).then_inc(S["consts_made"], 1)
            pool.memset(ones_b[:, :], 1.0).then_inc(S["consts_made"], 1)
            pool.memset(lnb[:, :], 10 * math.log(2.0)).then_inc(S["consts_made"], 1)
            pool.wait_ge(S["xuse"], NCH - 2)
            pool.memset(xc[:, 1, CH - 1, :], 0.0).then_inc(S["xpad"], 1)
            pool.wait_ge(S["deg_c"], 1)
            pool.memset(zT[:, :, :], 0.0).then_inc(S["zclear"], 1)
            pool.wait_ge(S["t_done"], 1)

            def fast():
                for s in range(2):
                    pool_group(pool, s, 0, s)
                with pool.Fori(1, NG // 2) as it:
                    pool_group(pool, it * 2, it, 0)
                    pool_group(pool, it * 2 + 1, it, 1)
                pool_group(pool, NG - 1, NG // 2, 0)
                pool_group(pool, NG, NG // 2, 1, TAILT)

            def general():
                def tile(i):
                    pool.wait_ge(S["g_idx"], i * 48 + 48)
                    wait(pool, S["g_sum"], i)
                    stand(pool)
                    pool.indirect_dma_start(G[:, 0, :], None, table,
                                            bass.IndirectOffsetOnAxis(ap=idx[:, 0, 0:1], axis=0)
                                            ).then_inc(S["g_gat"], 16)
                    pool.wait_ge(S["g_copy"], i + 1)
                    stand(pool)
                    pool.indirect_dma_start(zsum, bass.IndirectOffsetOnAxis(ap=g_tgt_i, axis=0), g_sum, None,
                                            compute_op=ALU.add).then_inc(S["g_sc"], 16)
                    pool.wait_ge(S["g_sc"], i * 16 + 16)

                pool.wait_ge(S["g_clear"], 16 * (NCH + 3))
                tile(0)
                with pool.Fori(1, ET) as i:
                    tile(i)

            choose(pool, fast, general)

        @block.scalar
        def _(act):
            def t_first(c, it, s):
                act.wait_ge(S[f"xin{s}"], it * 16 + 16 * (NCH // 2) + 16)
                wait(act, S["t_lo"], c - 1)
                for k in range(CH):
                    n = c * CH + k
                    last = nc.scalar.activation(tc[:, s, k, :], xc[:, s, k, :], ACT.Identity,
                                                scale=c_[:, ds(n, 1)], bias=cb[:, ds(n, 1)])
                    last.then_inc(S["t_raw"], 1)
                act.wait_ge(S["t_raw"], c * CH + CH)
                act.nop().then_inc(S["xuse"], 1)
                wait(act, S[f"t_out{s}"], it * 16)
                nc.scalar.activation(tb[:, s, :, 0:D], tc[:, s, :, :], ACT.Copy).then_inc(S["t_hi"], 1)

            def t_second(c, s):
                act.wait_ge(S["t_r1"], c + 1)
                nc.scalar.activation(tb[:, s, :, D:2 * D], tc[:, s, :, :], ACT.Copy).then_inc(S["t_mid"], 1)

            act.preload_act_table_set("natural_log_exp_and_others")

            def guess(v, to, scale=1.0, bias=0.0):
                nc.scalar.activation(to, v, ACT.Ln, scale=scale).then_inc(S["colg"], 1)
                n[0] += 1
                act.wait_ge(S["colg"], n[0])
                nc.scalar.activation(to, to, ACT.Exp, scale=-0.5, bias=bias).then_inc(S["colg"], 1)
                n[0] += 1

            n = [0]
            act.wait_ge(S["consts_made"], 3)
            act.wait_ge(S["cols"], 1)
            guess(deg[:, :], a_gd)
            guess(a_var, a_gs)
            act.wait_ge(S["cols"], 10)
            guess(a_m, a_gn, 2.0 ** 20, lnb[:, :])
            act.wait_ge(S["cols"], NCOLS)
            t_first(0, 0, 0)
            t_first(1, 0, 1)
            t_second(0, 0)
            with act.Fori(1, NCH // 2 - 1) as it:
                t_first(it * 2, it, 0)
                t_second(it * 2 - 1, 1)
                t_first(it * 2 + 1, it, 1)
                t_second(it * 2, 0)
            t_first(NCH - 2, NCH // 2 - 1, 0)
            t_second(NCH - 3, 1)
            act.wait_ge(S["xin_last"], 32)
            t_first(NCH - 1, NCH // 2 - 1, 1)
            t_second(NCH - 2, 0)
            t_second(NCH - 1, 1)

            def kv(i, it, s):
                if not constant(i, NT - 1):
                    act_kv_transposed(act, i + 1, 1 - s)
                act_kv(act, i, s)
                if not (constant(i, NT - 1) or constant(i, NT - 2)):
                    act_kv_scale(act, i + 2, it + 1, s)

            def a_first(j, it, s):
                act_a_scale(act, j, it, s)
                act_a_transposed(act, j)
                act_a_relu(act, j)
                act_a_norms(act, j)
                act_a_u(act, j, s)

            def pair(j, it, s):
                more = not constant(j, NP - 1)
                if more:
                    act_a_scale(act, j + 1, it + s, 1 - s)
                act_b_transposed(act, j)
                act_b_gate1(act, j)
                act_b_first(act, j, (0, 1))
                act_b_gate2(act, j)
                act_b_first(act, j, (2, 3, 4, 5))
                if more:
                    act_a_transposed(act, j + 1)
                    act_a_relu(act, j + 1)
                act_b_second(act, j)
                if more:
                    act_a_norms(act, j + 1)
                    act_a_u(act, j + 1, 1 - s)

            def keys():
                act.wait_ge(S["zclear"], 1)
                act_kv_scale(act, 0, 0, 0)
                act_kv_scale(act, 1, 0, 1)
                act_kv_transposed(act, 0, 0)
                tiles_in_pairs(act, kv)
                act.wait_ge(S["mid_d"], 11)
                a_first(0, 0, 0)

            def fast():
                keys()
                pairs_with_groups(act, pair)
                for j in range(NPL, NP):
                    pair(j, j // 2, j % 2)

            def general():
                keys()
                pairs_alone(act, pair)

            choose(act, fast, general)

        @block.vector
        def _(dve):
            V = nc.vector

            def chain(signal):
                n = [0]

                def run(ins):
                    ins.then_inc(S[signal], 1)
                    n[0] += 1
                    dve.wait_ge(S[signal], n[0])
                return run

            step = chain("base_f")
            dve.wait_ge(S["dst"], 16)
            step(V.tensor_copy(dst_f, dst_i))
            step(V.tensor_copy(base_f, dst_f[0:1, ::K]))
            step(V.tensor_copy(base_i[:, :], base_f))
            dve.wait_ge(S["base_b"], 1)
            bases = pb[7][:, 0:NG + 1]
            step(V.tensor_tensor(dst_f[:, 0:NG * K].rearrange("p (g k) -> p g k", k=K),
                                 dst_f[:, 0:NG * K].rearrange("p (g k) -> p g k", k=K),
                                 bases[:, 0:NG].unsqueeze(2).to_broadcast([P, NG, K]), ALU.subtract))
            step(V.tensor_scalar(dst_f[:, NG * K:ET], dst_f[:, NG * K:ET], bases[:, NG:NG + 1], None,
                                 ALU.subtract))
            step(V.tensor_copy(dloc[:, :], dst_f))
            step(V.tensor_reduce(mx[:, 0:1], dst_f, AX, ALU.max))
            step(V.tensor_reduce(mx[:, 1:2], dst_f, AX, ALU.min))
            step(V.tensor_scalar(mx[:, 1:2], mx[:, 1:2], -1.0, None, ALU.mult))
            step(V.tensor_scalar(mx[:, 2:3], mx[:, 0:1], -(W - 1.0), mx[:, 1:2], ALU.add, ALU.max))
            dve.wait_ge(S["const"], 64)
            step(V.tensor_tensor(lim, lim, base_f, ALU.subtract))
            step(V.tensor_reduce(mx[0:1, 3:4], lim, AX, ALU.max))
            V.tensor_tensor(mx[0:1, 2:3], mx[0:1, 2:3], mx[0:1, 3:4], ALU.max).then_inc(S["range_v"], 1)
            dve.wait_ge(S["range_t"], 1)
            step = chain("flag_c")
            step(V.tensor_reduce(mx[0:1, 4:5], pb[7][0:1, 256:256 + P], AX, ALU.max))
            step(V.tensor_scalar(mx[0:1, 5:6], mx[0:1, 4:5], 0.0, None, ALU.is_gt))
            V.tensor_copy(flag_i[:, :], mx[0:1, 5:6]).then_inc(S["flag"], 1)
            V.tensor_copy(iota_w[:, :], iota[:, 0:W]).then_inc(S["iota_w"], 1)
            dve.wait_ge(S["iota_w"], 1)
            dve.wait_ge(S["consts_made"], 3)

            def degrees_fast():
                V.memset(deg_row, 0.0).then_inc(S["deg_zero"], 1)
                dve.wait_ge(S["deg_zero"], 1)

                def onehot(g, s, k=K):
                    wait(dve, S["deg_ps"], g - 1)
                    V.tensor_tensor(oh[:, s, 0:k, :], dloc[:, ds(g * K, k)].unsqueeze(2).to_broadcast([P, k, W]),
                                    iota_w[:, :].unsqueeze(1).to_broadcast([P, k, W]),
                                    ALU.is_equal).then_inc(S["deg_oh"], 1)

                def add(g, s):
                    dve.wait_ge(S["deg_ps"], g + 1)
                    wait(dve, S["deg_add"], g)
                    b = dve.value_load(base_i[0:1, ds(g, 1)], min_val=0, max_val=NPAD)
                    V.tensor_tensor(deg_row[0:1, ds(b, W)], deg_row[0:1, ds(b, W)],
                                    pb[s][0:1, 0:W], ALU.add).then_inc(S["deg_add"], 1)

                onehot(0, 0)
                onehot(1, 1)
                add(0, 0)
                with dve.Fori(1, NG // 2) as it:
                    onehot(it * 2, 0)
                    add(it * 2 - 1, 1)
                    onehot(it * 2 + 1, 1)
                    add(it * 2, 0)
                onehot(NG - 1, 0)
                add(NG - 2, 1)
                onehot(NG, 1, TAILT)
                add(NG - 1, 0)
                add(NG, 1)

            def degrees_general():
                step = chain("g_ab")
                step(V.tensor_scalar(g_hi_i, dst_i, 7, None, ALU.logical_shift_right))
                step(V.tensor_scalar(g_lo_i, dst_i, 127, None, ALU.bitwise_and))
                step(V.tensor_copy(g_hi, g_hi_i))
                step(V.tensor_copy(g_lo, g_lo_i))

                def onehots(i):
                    wait(dve, S["g_dps"], i)
                    for of, to, n in ((g_hi, g_oha, NT), (g_lo, g_ohb, P)):
                        V.tensor_tensor(to[:, :, 0:n], of[:, ds(i * GD, GD)].unsqueeze(2).to_broadcast([P, GD, n]),
                                        iota[:, 0:n].unsqueeze(1).to_broadcast([P, GD, n]),
                                        ALU.is_equal).then_inc(S["g_oh"], 1)

                onehots(0)
                with dve.Fori(1, ET // GD) as i:
                    onehots(i)

            def stats(c, it, s, n0=0):
                dve.wait_ge(S[f"xin{s}"], it * 16 + 16)
                for k in range(CH):
                    V.bn_stats(bns[:, k, :], xc[:, s, k, :]).then_inc(S["bn"], 1)
                dve.wait_ge(S["bn"], c * CH + CH)
                stand(dve)
                for k in range(CH):
                    V.bn_aggr(bna[:, k, :], bns[:, k, :]).then_inc(S["bna"], 1)
                dve.wait_ge(S["bna"], c * CH + CH)
                V.tensor_copy(stat[:, ds(c * CH, CH), :], bna[:, :, :]).then_inc(S["xuse"], 1)
                dve.wait_ge(S["xuse"], c + 1)

            stats(0, 0, 0)
            stats(1, 0, 1)
            with dve.Fori(1, NCH // 2 - 1) as it:
                stats(it * 2, it, 0)
                stats(it * 2 + 1, it, 1)
            stats(NCH - 2, NCH // 2 - 1, 0)
            dve.wait_ge(S["xin_last"], 16)
            stats(NCH - 1, NCH // 2 - 1, 1)

            dve.wait_ge(S["weights"], 16 * NWEIGHTS)
            wh = wkv[:, :, :].rearrange("p c (h d) -> p (c h) d", d=DH)
            step = chain("wcent")
            step(V.tensor_reduce(wmean, wh, AX, ALU.add))
            step(V.tensor_scalar(wmean, wmean, 1.0 / DH, None, ALU.mult))
            step(V.tensor_tensor(wh, wh, wmean.unsqueeze(2).to_broadcast([P, 32, DH]), ALU.subtract))

            choose(dve, degrees_fast, degrees_general)

            dve.wait_ge(S["deg_t"], 1)
            V.tensor_scalar(deg[:, :], pb[6][:, 0:NT], 1.0, None, ALU.add).then_inc(S["deg_c"], 1)

            mean, var = stat[:, :, 0], stat[:, :, 1]
            n = [0]

            def step(ins):
                ins.then_inc(S["cols"], 1)
                n[0] += 1
                dve.wait_ge(S["cols"], n[0])

            def polish(v, guess, to):
                dve_polish(dve, v, guess, a_t, to, S["cols"], n[0])
                n[0] += 3

            dve.wait_ge(S["deg_c"], 1)
            step(V.tensor_scalar(a_var, var, EPS_LN, None, ALU.add))
            dve.wait_ge(S["colg"], 4)
            polish(deg[:, :], a_gd, a_di)
            polish(a_var, a_gs, a_sd)
            step(V.tensor_tensor(a_t, var, a_sd, ALU.mult))
            step(V.scalar_tensor_tensor(a_t, a_t, float(D), a_sd, ALU.mult, ALU.mult))
            step(V.tensor_scalar(a_m, a_t, EPS_NRM ** 2, None, ALU.max))
            dve.wait_ge(S["colg"], 6)
            polish(a_m, a_gn, a_rn)
            step(V.tensor_tensor(dsq[:, :], deg[:, :], a_di, ALU.mult))
            step(V.tensor_tensor(a_m, a_m, a_rn, ALU.mult))
            step(V.tensor_tensor(q[:, :], a_m, dsq[:, :], ALU.mult))
            step(V.tensor_tensor(q2[:, :], q[:, :], q[:, :], ALU.mult))
            step(V.tensor_scalar(q264[:, :], q2[:, :], 1.0 / DH, None, ALU.mult))
            step(V.tensor_scalar(tiny2[:, :], deg[:, :], EPS_NRM ** 2, None, ALU.mult))
            step(V.tensor_tensor(a_t, a_sd, a_rn, ALU.mult))
            step(V.tensor_tensor(c_[:, :], a_t, a_di, ALU.mult))
            step(V.scalar_tensor_tensor(cb[:, :], mean, -1.0, c_[:, :], ALU.mult, ALU.mult))
            step(V.tensor_tensor(cD[:, :], c_[:, :], deg[:, :], ALU.mult))
            step(V.tensor_tensor(cbD[:, :], cb[:, :], deg[:, :], ALU.mult))
            assert n[0] == NCOLS

            def rest(c, s):
                dve.wait_ge(S["t_hi"], c + 1)
                V.tensor_tensor(tc[:, s, :, :], tc[:, s, :, :], tb[:, s, :, 0:D],
                                ALU.subtract).then_inc(S["t_r1"], 1)

            def third(c, s):
                dve.wait_ge(S["t_mid"], c + 1)
                V.tensor_tensor(tb[:, s, :, 2 * D:3 * D], tc[:, s, :, :], tb[:, s, :, D:2 * D],
                                ALU.subtract).then_inc(S["t_lo"], 1)

            rest(0, 0)
            rest(1, 1)
            third(0, 0)
            with dve.Fori(1, NCH // 2) as it:
                rest(it * 2, 0)
                third(it * 2 - 1, 1)
                rest(it * 2 + 1, 1)
                third(it * 2, 0)
            third(NCH - 1, 1)
            dve.wait_ge(S["t_lo"], NCH)

            def clear(general):
                V.memset(bd, 0.0).then_inc(S["zero_l"], 1)
                dve.wait_ge(S["zclear"], 1)

            def pad_kv(i):
                if constant(i, NT - 3):
                    dve.wait_ge(S["td"], 2 * (NT - 2))
                    V.memset(xk[:, 1, :], 0.0).then_inc(S["xkpad"], 1)

            def pad_a(j):
                if constant(j, NP - 3):
                    dve.wait_ge(S["y"], 6 * (NP - 2))
                    V.memset(xf[:, 1, :], 0.0).then_inc(S["xfpad"], 1)

            def a_all(j, s, groups):
                dve_a_sum(dve, j, groups)
                dve_a_v(dve, j)
                dve_a_y(dve, j, s)

            def tiles(kv):
                kv(0, 0, 0)
                kv(1, 0, 1)
                with dve.Fori(1, NP - 2) as it:
                    kv(it * 2, it, 0)
                    kv(it * 2 + 1, it, 1)
                for i in range(NT - 4, NT):
                    kv(i, i // 2, i % 2)

            def pair(j, it, s, grouped):
                more = not constant(j, NP - 1)
                g0 = group_at(j, it, s, 0)[0]
                slot = s
                pad_a(j)
                if grouped:
                    dve_onehot(dve, g0 + 1, 1 - slot)
                    dve_group_add(dve, g0, slot)
                dve_b_gate1(dve, j)
                dve_b_gate2(dve, j)
                dve_b_gate3(dve, j)
                if more:
                    dve_a_sum(dve, j + 1, g0 + 1 if grouped else None)
                if grouped:
                    dve_onehot(dve, g0 + 2, slot)
                    dve_group_add(dve, g0 + 1, 1 - slot)
                dve_b_weights(dve, j)
                if more:
                    dve_a_v(dve, j + 1)
                dve_b_second(dve, j)
                if grouped:
                    dve_onehot(dve, g0 + 3, 1 - slot)
                    dve_group_add(dve, g0 + 2, slot)
                if more:
                    dve_a_y(dve, j + 1, 1 - s)
                dve_b_out(dve, j, it, s)

            def fast():
                clear(False)
                dve_onehot(dve, 0, 0)

                def kv(i, it, s):
                    dve_onehot(dve, i + 1, 1 - s)
                    pad_kv(i)
                    dve_kv(dve, i, s)
                    dve_group_add(dve, i, s)

                tiles(kv)
                dve_mid(dve)
                a_all(0, 0, GP1)
                pairs_with_groups(dve, lambda j, it, s: pair(j, it, s, True))
                dve_onehot(dve, NG, 1, TAILT)
                dve_group_add(dve, NG - 1, 0)
                dve_group_add(dve, NG, 1)
                dve.wait_ge(S["acc"], NG + 1)
                for j in range(NPL, NP):
                    pair(j, j // 2, j % 2, False)

            def general():
                V.memset(tc[:, 0, :, :], 0.0).then_inc(S["g_zero"], 1)
                dve.wait_ge(S["zclear"], 1)
                dve.wait_ge(S["g_clear"], 16 * (NCH + 3))

                def tile(i):
                    ch = [0]

                    def step(ins):
                        ins.then_inc(S["g_ch"], 1)
                        ch[0] += 1
                        dve.wait_ge(S["g_ch"], i * 7 + ch[0])

                    dve.wait_ge(S["g_idx"], i * 48 + 48)
                    step(V.tensor_copy(g_row, g_row_i))
                    step(V.tensor_copy(g_dst, idx[:, 0, 1:2]))
                    V.tensor_scalar(g_eq, g_row, g_dst, None, ALU.is_equal).then_inc(S["g_e"], 1)
                    step(V.scalar_tensor_tensor(g_cmp, g_row, g_dst, low, ALU.is_equal, ALU.mult))
                    step(V.tensor_reduce(g_cnt, g_cmp, AX, ALU.max))
                    step(V.tensor_tensor(g_tgt, trash, g_dst, ALU.subtract))
                    step(V.scalar_tensor_tensor(g_tgt, g_tgt, g_cnt, g_dst, ALU.mult, ALU.add))
                    step(V.tensor_copy(g_tgt_i, g_tgt))
                    dve.wait_ge(S["g_sum"], i + 1)
                    V.tensor_copy(g_sum, pb[0][:, 0:D]).then_inc(S["g_copy"], 1)

                tile(0)
                with dve.Fori(1, ET) as i:
                    tile(i)

                def back(n):
                    dve.wait_ge(S["g_ztr"], n + 1)
                    V.tensor_copy(zT[:, :, ds(n * P, P)],
                                  pb[1][:, 0:D].rearrange("p (c n) -> p c n", c=2)).then_inc(S["g_zcp"], 1)

                back(0)
                with dve.Fori(1, NT) as n:
                    back(n)
                dve.wait_ge(S["g_zcp"], NT)
                V.memset(bd, 0.0).then_inc(S["zero_l"], 1)

                def kv(i, it, s):
                    pad_kv(i)
                    dve_kv(dve, i, s)

                tiles(kv)
                dve_mid(dve)
                a_all(0, 0, None)
                pairs_alone(dve, lambda j, it, s: pair(j, it, s, False))

            choose(dve, fast, general)

        @block.tensor
        def _(pe):
            T = nc.tensor
            pe.wait_ge(S["consts_made"], 3)
            pe.wait_ge(S["base_f"], 2)
            T.matmul(pb[7][:, 0:NG + 1], ones[0:1, :], base_f, start=True, stop=True).then_inc(S["base_b"], 1)
            pe.wait_ge(S["const"], 64)
            pe.wait_ge(S["range_v"], 1)
            T.transpose(pb[7][0:1, 256:256 + P], mx[:, 2:3], ident[:, :]).then_inc(S["range_t"], 1)

            def degrees_fast():
                def count(g, s, k=K):
                    pe.wait_ge(S["deg_oh"], g + 1)
                    wait(pe, S["deg_add"], g - 1)
                    for j in range(k):
                        last = T.matmul(pb[s][0:1, 0:W], ones_b[:, :], oh[:, s, j, :],
                                        start=(j == 0), stop=(j == k - 1))
                    last.then_inc(S["deg_ps"], 1)

                count(0, 0)
                count(1, 1)
                with pe.Fori(1, NG // 2) as it:
                    count(it * 2, 0)
                    count(it * 2 + 1, 1)
                count(NG - 1, 0)
                count(NG, 1, TAILT)
                pe.wait_ge(S["deg_98"], 16)
                T.transpose(pb[6][:, 0:NT], deg_98, ident[0:NT, 0:NT]).then_inc(S["deg_t"], 1)

            def degrees_general():
                def count(i):
                    pe.wait_ge(S["g_oh"], i * 2 + 2)
                    for k in range(GD):
                        last = T.matmul(pb[6][:, 0:NT], g_ohb[:, k, :], g_oha[:, k, 0:NT], start=first and k == 0,
                                        stop=False, skip_group_check=True)
                    last.then_inc(S["g_dps"], 1)

                first = True
                count(0)
                first = False
                with pe.Fori(1, ET // GD) as i:
                    count(i)
                pe.wait_ge(S["g_dps"], ET // GD)
                T.nop().then_inc(S["deg_t"], 1)

            choose(pe, degrees_fast, degrees_general)

            def start_sums():
                pe.wait_ge(S["zero_l"], 1)
                pe.wait_ge(S["wcent"], 3)
                for bank in (4, 5):
                    T.matmul(pb[bank][:, :], bd[:, 0, :], wkv[:, 0, 0:INNER], start=True, stop=False,
                             skip_group_check=True).then_inc(S["psum0"], 1)
                pe_kv_transpose(pe, 0, 0)

            def tiles(grouped):
                def kv(i, it, s):
                    if not constant(i, NT - 1):
                        pe_kv_transpose(pe, i + 1, 1 - s)
                    pe_kv(pe, i, s)
                    if not constant(i, 0):
                        pe_dots(pe, i - 1, 1 - s)
                    pe_hth(pe, i, s)
                    if grouped:
                        pe_group(pe, i, it, s)

                tiles_in_pairs(pe, kv)
                pe_dots(pe, NT - 1, 1)

            def pair(j, it, s, grouped):
                more = not constant(j, NP - 1)
                at_ = [group_at(j, it, s, n) for n in range(GPP)]
                pe_b_transpose(pe, j)
                if grouped:
                    pe_group(pe, *at_[0])
                pe_b_first(pe, j)
                if more:
                    pe_a_transpose(pe, j + 1)
                if grouped:
                    pe_group(pe, *at_[1])
                pe_b_weights(pe, j)
                if more:
                    pe_a(pe, j + 1)
                pe_b_second(pe, j)
                if grouped:
                    pe_group(pe, *at_[2])
                pe_b_out(pe, j)

            def fast():
                start_sums()
                tiles(True)
                pe_mid(pe)
                pe_a_transpose(pe, 0)
                pe_a(pe, 0)
                pairs_with_groups(pe, lambda j, it, s: pair(j, it, s, True))
                pe_group(pe, NG - 1, NG // 2, 0)
                pe_group(pe, NG, NG // 2, 1, TAILT)
                for j in range(NPL, NP):
                    pair(j, j // 2, j % 2, False)

            def general():
                def tile(i):
                    pe.wait_ge(S["g_gat"], i * 16 + 16)
                    pe.wait_ge(S["g_e"], i + 1)
                    wait(pe, S["g_copy"], i)
                    for part in range(3):
                        last = T.matmul(pb[0][:, 0:D], g_eq, G[:, 0, part * D:part * D + D],
                                        start=(part == 0), stop=(part == 2))
                    last.then_inc(S["g_sum"], 1)

                tile(0)
                with pe.Fori(1, ET) as i:
                    tile(i)

                def back(n):
                    pe.wait_ge(S["g_zld"], n * 16 + 16)
                    wait(pe, S["g_zcp"], n)
                    for c in range(2):
                        last = T.transpose(pb[1][:, c * P:c * P + P], g_z[:, c * P:c * P + P], ident[:, :])
                    last.then_inc(S["g_ztr"], 1)

                back(0)
                with pe.Fori(1, NT) as n:
                    back(n)
                start_sums()
                tiles(False)
                pe_mid(pe)
                pe_a_transpose(pe, 0)
                pe_a(pe, 0)
                pairs_alone(pe, lambda j, it, s: pair(j, it, s, False))

            choose(pe, fast, general)


def kernel(x, src, dst, L0_gnn_W_gcn, L0_gnn_b_gcn, L0_gnn_W_V, L0_mix_w_qkv, L0_mix_w_out, L0_mix_b_out,
           L0_ffn_sW1, L0_ffn_sb1, L0_ffn_sW2, L0_ffn_sb2, L0_ffn_sW3, L0_ffn_sb3, L0_ffn_eW1, L0_ffn_eb1,
           L0_ffn_eW2, L0_ffn_eb2, L0_ffn_eW3, L0_ffn_eb3, L0_ffn_gW, L0_ffn_gb):
    import concourse.bacc as _bacc
    from concourse.bass_utils import run_bass_kernel_spmd as _run

    def edge_tiles(a, fill):
        a = np.asarray(a)
        whole = a[:NG * GE].reshape(NG, P, K).transpose(1, 0, 2).reshape(P, NG * K)
        tail = np.full(TAILT * P, fill, a.dtype)
        tail[:E - NG * GE] = a[NG * GE:]
        return np.concatenate([whole, tail.reshape(TAILT, P).T], axis=1)

    dst_t = edge_tiles(dst, N)
    limit = np.zeros((1, NG + 1), np.float32)
    for j in range(NPL):
        for n in range(GPP):
            limit[0, GP1 + GPP * j + n] = 2 * P * (j + 1 + (n > 0))
    limit[0, GP1 + GPP * NPL:] = 2 * P * (NPL + 1)
    pick = np.zeros((5, 2, P), np.float32)
    for e in range(4):
        pick[e, e // 2, (e % 2) * 64:(e % 2) * 64 + 64] = 1.0
    w_qkv = np.asarray(L0_mix_w_qkv)
    arrays = {
        "x": x, "src_t": edge_tiles(src, 0), "dst_t": dst_t, "dst_rows": dst_t.T,
        "w_kvT": w_qkv[INNER:].T, "w_q": w_qkv[:INNER], "w_oT": np.asarray(L0_mix_w_out).T,
        "w_V": L0_gnn_W_V, "w_gcn": L0_gnn_W_gcn, "b_gcn": np.asarray(L0_gnn_b_gcn)[None],
        "b_out": np.asarray(L0_mix_b_out)[None], "sW1": L0_ffn_sW1, "eW1": L0_ffn_eW1, "sW2": L0_ffn_sW2,
        "eW2": L0_ffn_eW2, "sW3": L0_ffn_sW3, "eW3": np.asarray(L0_ffn_eW3).reshape(4 * 64, D),
        "gW": L0_ffn_gW, "gb": np.asarray(L0_ffn_gb)[None],
        "h_bias": np.concatenate([np.asarray(a).reshape(-1, P) for a in (
            L0_ffn_sb1, L0_ffn_eb1, L0_ffn_sb2, L0_ffn_eb2)], axis=0).T,
        "o_bias": np.concatenate([np.asarray(L0_ffn_eb3), np.asarray(L0_ffn_sb3)[None]], axis=0),
        "c_ident": np.eye(P, dtype=np.float32), "c_iota": np.arange(P, dtype=np.float32)[None],
        "c_rank": np.array([[4, 3, 2, 1, 4, 3, 2, 1]], np.float32), "c_limit": limit, "c_pick": pick,
        "c_low": np.tril(np.ones((P, P), np.float32), -1),
        "c_trash": (NPAD + np.arange(P, dtype=np.float32))[:, None],
    }
    nc = _bacc.Bacc("TRN2", target_bir_lowering=False, num_devices=1)
    feed, args = {}, []
    for name, a in arrays.items():
        a = np.ascontiguousarray(a)
        feed[f"in_{name}"] = a
        args.append(nc.dram_tensor(f"in_{name}", a.shape, mybir.dt.from_np(a.dtype), kind="ExternalInput").ap())
    args.append(nc.dram_tensor("out_rows", (N, D), F32, kind="ExternalOutput").ap())
    build(nc, *args)
    return _run(nc, [feed], core_ids=[0]).results[0]["out_rows"]
```

```python
import math
from contextlib import ExitStack

import concourse.bass as bass
import numpy as np
from concourse import mybir
from concourse.bass import ds

F32, BF16, I32 = mybir.dt.float32, mybir.dt.bfloat16, mybir.dt.int32
ALU = mybir.AluOpType
ACT = mybir.ActivationFunctionType
AX = mybir.AxisListType.X

N, E = 12500, 212500
P = 128
NT = -(-N // P)
NPAD = NT * P
LAST = N - (NT - 1) * P
D = 256
K = 7
GE = K * P
NG = E // GE
TAILT = -(-(E - NG * GE) // P)
ET = NG * K + TAILT
W = 64
ZN = NPAD + W
HEADS, DH = 8, 64
INNER = HEADS * DH
NP = NT // 2
CH = 7
NCH = NT // CH
GP1 = NT
GPP = 3
NPL = (NG - GP1) // GPP
EPS_LN = 1e-5
EPS_NRM = 1e-12
BETA = 0.1
R9 = 3 * 3 * 5
LB = 8
WH = -(-W // LB) + 1
DA = -(-NPAD // (LB * P))
BG = 3
NB = NG // BG
NCA = 13
T_ACT = 3
NWEIGHTS = 18


def wait(e, sem, value):
    if isinstance(value, int) and value <= 0:
        return
    e.wait_ge(sem, value)


def build(nc, x, src_t, dst_t, dst_rows, w_kvT, w_q, w_oT, w_V, w_gcn, b_gcn, b_out, sW1, eW1, sW2, eW2,
          sW3, eW3, gW, gb, h_bias, o_bias, c_ident, c_iota, c_rank, c_limit, c_pick, c_parts, c_low, c_trash, out):
    table = nc.dram_tensor("table", (NPAD, 3 * D), BF16, kind="Internal").ap()
    zsum = nc.dram_tensor("zsum", (NPAD + P, D), F32, kind="Internal").ap()
    ctx = ExitStack()
    with ctx:
        def sb(name, shape, dt=F32):
            return ctx.enter_context(nc.sbuf_tensor(name, shape, dt))

        def sem(name):
            return ctx.enter_context(nc.semaphore(name))

        zT = sb("zT", [P, 2, ZN])
        G = sb("G", [P, 2 * K, 3 * D], BF16)
        idx = sb("idx", [P, 2, K], I32)
        oh = sb("oh", [P, 2, K, W], BF16)
        dloc = sb("dloc", [P, ET], BF16)
        base_i = sb("base_i", [1, NG + 1], I32)
        flag_i = sb("flag_i", [1, 1], I32)
        ident = sb("ident", [P, P])
        iota = sb("iota", [P, P])
        iota_w = sb("iota_w", [P, W], BF16)
        ones = sb("ones", [P, P])
        ones_b = sb("ones_b", [P, 1], BF16)
        rank = sb("rank", [P, 8])
        bB = sb("bB", [P, D])
        boB = sb("boB", [P, D])
        gbB = sb("gbB", [P, 8])
        hb = sb("hb", [P, 9])
        ob = sb("ob", [R9, D])
        ob9 = sb("ob9", [R9, D], BF16)
        parts = sb("parts", [R9, 3])
        pick = sb("pick", [R9, 2, P])
        pick_b = sb("pick_b", [R9, 2, P], BF16)
        ident_b = sb("ident_b", [P, P], BF16)
        wkv = sb("wkv", [P, 2, 2 * INNER])
        wg = sb("wg", [P, 2, D])
        mp = sb("mp", [P, 2, 2 * D])
        w1 = sb("w1", [P, 2, 6, P])
        w2s = sb("w2s", [P, 2, P])
        w2e = sb("w2e", [P, 4, 64])
        w3 = sb("w3", [P, 3, D])
        gw = sb("gw", [P, 2, 4])
        deg, dsq, c_, cb, cD, cbD, q, q2, q264, tiny2 = (
            sb(n, [P, NT]) for n in ("deg", "dsq", "c", "cb", "cD", "cbD", "q", "q2", "q264", "tiny2"))
        stat = sb("stat", [P, NT, 2])
        lnb = sb("lnb", [P, 1])
        bns = sb("bns", [P, CH, 6])
        bna = sb("bna", [P, CH, 2])
        high_i = sb("high_i", [1, NG + 1], I32)
        counts = sb("counts", [LB, 2, BG * WH])
        rsum, rneg, rsq = (sb(n, [P, CH]) for n in ("rsum", "rneg", "rsq"))

        arena = sb("arena", [P, 9856])
        at = [0]

        def cut(n, *shape):
            v = arena[:, at[0]:at[0] + n]
            at[0] += n
            if len(shape) == 2:
                v = v.rearrange("p (a b) -> p a b", a=shape[0])
            if len(shape) == 3:
                v = v.rearrange("p (a b c) -> p a b c", a=shape[0], b=shape[1])
            return v

        xc = cut(2 * CH * D, 2, CH, D)
        tc = cut(2 * CH * D, 2, CH, D)
        rc = cut(CH * D, CH, D)
        tb = G[:, :, :].rearrange("p (s k) f -> p s k f", s=2)
        at[0] = 0
        xk, tk, dk = cut(512, 2, D), cut(512, 2, D), cut(512, 2, D)
        ttk = cut(512, 2, 2, P)
        sq = cut(1024, 16, DH)
        ks, vs = cut(1024, 2, INNER), cut(1024, 2, INNER)
        msum, mm, pr, al, al2, kr, kn = cut(16), cut(16), cut(8), cut(8), cut(8), cut(8), cut(8)
        wq_m, wo_m, r_m = cut(1024, 4, D), cut(1024, 4, D), cut(1024, 4, D)
        hh, wv_m = cut(512, 2, D), cut(512, 2, D)
        bd = cut(512, 4, P)
        assert at[0] <= 9856
        at[0] = 0
        xf = cut(1024, 4, D)
        tf, ttf, ag = cut(512, 2, D), cut(512, 2, 2 * P), cut(512, 2, 2 * P)
        vv, rr = cut(512, 2, D), cut(512, 2, D)
        sqf = cut(256)
        yy = cut(1024, 2, 2, D)
        uu = cut(512, 2, D)
        uT = cut(512, 2, 2 * P)
        h1 = cut(1536, 6, 2 * P)
        h2 = cut(768, 3, 2 * P)
        oo = cut(1024, 2, 2, D)
        wT = cut(128).bitcast(BF16)
        lg, e_g, gt, o1, g2, o2, t8 = (cut(8, 2, 4) for _ in range(7))
        w5, w5r = cut(10, 2, 5), cut(10, 2, 5)
        w9 = cut(R9).bitcast(BF16).rearrange("p (t i j e) -> p t i j e", t=2, i=3, j=3)
        v2 = [cut(2) for _ in range(12)]
        ss, lo, rs0, nt_, inv, vr, rs1, rstd, nb_ = (cut(2) for _ in range(9))
        bnf = cut(12, 2, 6)
        mvf = cut(4, 2, 2)
        assert at[0] <= 9856

        zflat = zT[:, :, :].rearrange("p c n -> p (c n)")
        dst_i = zflat[:, 0:ET].bitcast(I32)
        dst_f = zflat[:, ET:2 * ET]
        part_i = zflat[:, 2 * ET:3 * ET].bitcast(I32)
        o = 3 * ET
        hi_b = zflat[:, o:o + (ET + 1) // 2].bitcast(BF16)[:, 0:ET]
        lo_b = zflat[:, o + (ET + 1) // 2:o + (ET + 1) // 2 * 2].bitcast(BF16)[:, 0:ET]
        o += (ET + 1) // 2 * 2
        base_f, lim, high_f = (zflat[0:1, o + 256 * k:o + 256 * k + NG + 1] for k in range(3))
        high_t = zflat[0:1, o + 768:o + 768 + NG + 1].bitcast(I32)
        mx = zflat[:, o + 1024:o + 1032]
        o += 1040
        deg_q = zflat[:, o:o + DA * LB]
        deg_98 = zflat[0:NT, o + DA * LB:o + DA * LB + P]
        assert o + DA * LB + P <= 2 * ZN
        oh_lo, oh_hi = (oh[:, :, :, :].rearrange("p s k w -> p s (k w)")[:, :, o:o + BG * K * n].rearrange(
            "p s (t n) -> p s t n", n=n) for o, n in ((0, LB), (BG * K * LB, WH)))
        deg_8 = arena[0:LB, 2 * CH * D:2 * CH * D + BG * DA * P].rearrange("p (k h) -> p k h", k=BG)
        junk = G[:, 9:14, :].rearrange("p k f -> p (k f)").bitcast(F32)[:, 0:CH * D].rearrange(
            "p (k d) -> p k d", k=CH)
        pb = [ctx.enter_context(nc.psum_tensor(f"bank{i}", [P, 512], F32)) for i in range(8)]
        AGG = [pb[s][:, 0:2 * W].rearrange("p (c w) -> p c w", c=2) for s in range(2)]

        S = {n: sem("s_" + n) for n in (
            "iota_w deg_c colg const weights dst xin0 xin1 xin_last xpad xuse0 xuse1 ast base_f base_b range_v range_t flag flag_c "
            "deg_zero deg_oh deg_ps deg_cp deg_add0 deg_add1 deg_add2 deg_sum deg_q deg_row deg_98 deg_t cols consts_made wcent "
            "bn bna t_done t_ra t_rp t_hi t_r1 t_mid t_lo t_out0 t_out1 zclear split zero_l psum0 "
            "idx0 idx1 gat0 gat1 oh agg acc "
            "kn xk0 xk1 xkpad td tr tt k_ps v_ps sq vs chain_kv ks dots hth mid_w mid_p mid_d "
            "rs stand_v stand_p stand_s xf0 xf1 xf2 xf3 xfpad tf ttr ttf ag p12 vv ssq rr y st nb u tru ut gates lg eg gap ed w5 wt wtc "
            "h1 h1e wb h2 h2e h2w pout oo st0 st1 "
            "g_idx g_gat g_e g_ch g_sum g_copy g_sc g_zero g_clear g_ztr g_zld g_zcp g_oh g_ab g_dps").split()}

        def stand(e):
            e.sem_inc(S[{"Pool": "stand_p", "SP": "stand_s"}.get(e.engine.name, "stand_v")], 1)

        def first_columns(of, engine, most):
            return nc.values_load_multi_w_load_instructions(
                of, [engine], min_val=0, max_val=most,
                skip_runtime_bounds_check_because="destinations are nodes, and the table ends past them")[1]

        def sp_group_idx(sp, g, it, s, k=K):
            wait(sp, S[f"gat{s}"], it * (16 * K))
            stand(sp)
            sp.dma_start(idx[:, s, 0:k], src_t[:, ds(g * K, k)]).then_inc(S[f"idx{s}"], 16)

        def pool_group(pool, g, it, s, k=K):
            pool.wait_ge(S[f"idx{s}"], it * 16 + 16)
            wait(pool, S["agg"], g - 1)
            stand(pool)
            for j in range(k):
                pool.indirect_dma_start(G[:, s * K + j, :], None, table,
                                        bass.IndirectOffsetOnAxis(ap=idx[:, s, j:j + 1], axis=0)
                                        ).then_inc(S[f"gat{s}"], 16)

        def dve_onehot(dve, g, s, k=K):
            wait(dve, S["agg"], g - 1)
            nc.vector.tensor_tensor(oh[:, s, 0:k, :],
                                    dloc[:, ds(g * K, k)].unsqueeze(2).to_broadcast([P, k, W]),
                                    iota_w[:, :].unsqueeze(1).to_broadcast([P, k, W]),
                                    ALU.is_equal).then_inc(S["oh"], 1)

        def pe_group(pe, g, it, s, k=K):
            pe.wait_ge(S[f"gat{s}"], it * (16 * K) + 16 * k)
            pe.wait_ge(S["oh"], g + 1)
            wait(pe, S["acc"], g - 1)
            for j in range(k):
                for part in range(3):
                    for c in range(2):
                        o_ = part * D + c * P
                        last = nc.tensor.matmul(AGG[s][:, c, :], G[:, s * K + j, o_:o_ + P], oh[:, s, j, :],
                                                start=(j == 0 and part == 0 and c == 0),
                                                stop=(j == k - 1 and part == 2 and c == 1),
                                                skip_group_check=True)
            last.then_inc(S["agg"], 1)

        def dve_group_add(dve, g, s):
            dve.wait_ge(S["agg"], g + 1)
            wait(dve, S["acc"], g)
            b, = first_columns(base_i[0:1, ds(g, 1)], mybir.EngineType.DVE, NPAD)
            win = zT[:, :, ds(b, W)]
            nc.vector.tensor_tensor(win, win, AGG[s], ALU.add).then_inc(S["acc"], 1)

        def dve_polish(dve, v, guess, tmp, to, sem_, at_):
            V = nc.vector
            V.scalar_tensor_tensor(tmp, guess, -0.5, guess, ALU.mult, ALU.mult).then_inc(sem_, 1)
            dve.wait_ge(sem_, at_ + 1)
            V.tensor_tensor(tmp, tmp, v, ALU.mult).then_inc(sem_, 1)
            dve.wait_ge(sem_, at_ + 2)
            V.scalar_tensor_tensor(to, tmp, 1.5, guess, ALU.add, ALU.mult).then_inc(sem_, 1)
            dve.wait_ge(sem_, at_ + 3)

        KPS = (2, 7)

        def sp_kv_x(sp, i, s, last=False):
            wait(sp, S["td"], 2 * i - 2)
            stand(sp)
            if last:
                sp.wait_ge(S["xkpad"], 1)
            rows = LAST if last else P
            sp.dma_start(xk[0:rows, s, :], x[ds(i * P, rows), :]).then_inc(S[f"xk{s}"], 16)

        def act_kv_scale(act, i, it, s):
            act.wait_ge(S[f"xk{s}"], it * 16 + 16)
            wait(act, S["hth"], i - 1)
            nc.scalar.activation(tk[:, s, :], xk[:, s, :], ACT.Identity, scale=c_[:, ds(i, 1)],
                                 bias=cb[:, ds(i, 1)]).then_inc(S["td"], 1)
            nc.scalar.activation(dk[:, s, :], xk[:, s, :], ACT.Identity, scale=cD[:, ds(i, 1)],
                                 bias=cbD[:, ds(i, 1)]).then_inc(S["td"], 1)

        def pe_kv_transpose(pe, i, s):
            pe.wait_ge(S["td"], 2 * i + 2)
            wait(pe, S["tt"], i)
            for c in range(2):
                last = nc.tensor.transpose(pb[6][:, c * P:c * P + P],
                                           tk[:, s, c * P:c * P + P], ident[:, :])
            last.then_inc(S["tr"], 1)

        def act_kv_transposed(act, i, s):
            act.wait_ge(S["tr"], i + 1)
            wait(act, S["v_ps"], i - 1)
            nc.scalar.activation(ttk[:, s, :, :], pb[6][:, 0:256].rearrange(
                "p (c n) -> p c n", c=2), ACT.Copy).then_inc(S["tt"], 1)

        def pe_kv(pe, i, s):
            pe.wait_ge(S["tt"], i + 1)
            wait(pe, S["ks"], i - 1)
            for half, bank, signal in ((0, KPS[s], "k_ps"), (1, 3, "v_ps")):
                if half:
                    wait(pe, S["vs"], i)
                for c in range(2):
                    last = nc.tensor.matmul(pb[bank][:, :], ttk[:, s, c, :],
                                            wkv[:, c, half * INNER:(half + 1) * INNER],
                                            start=(c == 0), stop=(c == 1))
                last.then_inc(S[signal], 1)

        def act_kv(act, i, s):
            act.wait_ge(S["k_ps"], i + 1)
            wait(act, S["chain_kv"], 7 * i - 6)
            nc.scalar.activation(sq[:, 0:8, :].rearrange("p h d -> p (h d)"), pb[KPS[s]][:, :],
                                 ACT.Square).then_inc(S["sq"], 1)
            act.wait_ge(S["v_ps"], i + 1)
            nc.scalar.activation(sq[:, 8:16, :].rearrange("p h d -> p (h d)"), pb[3][:, :],
                                 ACT.Square).then_inc(S["sq"], 1)
            wait(act, S["dots"], i - 1)
            nc.scalar.activation(vs[:, s, :], pb[3][:, :], ACT.Copy).then_inc(S["vs"], 1)

        def act_kv_norm(act, i):
            act.wait_ge(S["chain_kv"], 7 * i + 3)
            nc.scalar.activation(kn, pr, ACT.Ln).then_inc(S["kn"], 1)
            act.wait_ge(S["kn"], 2 * i + 1)
            nc.scalar.activation(kr, kn, ACT.Exp, scale=-0.5).then_inc(S["kn"], 1)

        def dve_kv(dve, i, s):
            dve.wait_ge(S["sq"], 2 * i + 2)
            ch = S["chain_kv"]
            nc.vector.tensor_reduce(msum, sq, AX, ALU.add).then_inc(ch, 1)
            dve.wait_ge(ch, 7 * i + 1)
            nc.vector.tensor_scalar(mm, msum, q264[:, ds(i, 1)], EPS_LN, ALU.mult, ALU.add).then_inc(ch, 1)
            dve.wait_ge(ch, 7 * i + 2)
            nc.vector.tensor_tensor(pr, mm[:, 0:8], mm[:, 8:16], ALU.mult).then_inc(ch, 1)
            dve.wait_ge(S["kn"], 2 * i + 2)
            dve_polish(dve, pr, kr, al, al2, ch, 7 * i + 3)
            nc.vector.tensor_scalar(al, al2, q2[:, ds(i, 1)], None, ALU.mult).then_inc(ch, 1)
            dve.wait_ge(ch, 7 * i + 7)
            wait(dve, S["dots"], i - 1)
            nc.vector.tensor_tensor(ks[:, s, :].rearrange("p (h d) -> p h d", h=HEADS),
                                    pb[KPS[s]][:, :].rearrange("p (h d) -> p h d", h=HEADS),
                                    al.unsqueeze(2).to_broadcast([P, HEADS, DH]),
                                    ALU.mult).then_inc(S["ks"], 1)

        def pe_dots(pe, i, s):
            pe.wait_ge(S["ks"], i + 1)
            pe.wait_ge(S["vs"], i + 1)
            for h in range(4):
                last = nc.tensor.matmul(pb[4][:, h * P:h * P + P], vs[:, s, h * P:h * P + P],
                                        ks[:, s, h * P:h * P + P], start=False, stop=False,
                                        skip_group_check=True)
            last.then_inc(S["dots"], 1)

        def pe_hth(pe, i, s):
            nc.tensor.matmul(pb[5][:, 0:256], tk[:, s, 0:P], dk[:, s, :], start=False, stop=False,
                             skip_group_check=True)
            nc.tensor.matmul(pb[5][:, 256:384], tk[:, s, P:D], dk[:, s, P:D], start=False, stop=False,
                             skip_group_check=True).then_inc(S["hth"], 1)

        def sp_mid(sp):
            sp.dma_start(wv_m, w_V.rearrange("(c p) n -> p c n", p=P)).then_inc(S["mid_w"], 16)
            sp.dma_start(wq_m, w_q.rearrange("(h p) n -> p h n", p=P)).then_inc(S["mid_w"], 16)
            sp.dma_start(wo_m, w_oT.rearrange("(h p) n -> p h n", p=P)).then_inc(S["mid_w"], 16)

        def dve_mid(dve):
            mid = S["mid_d"]
            dve.wait_ge(S["hth"], NT)
            dve.wait_ge(S["dots"], NT)
            nc.vector.tensor_copy(hh[:, 0, :], pb[5][:, 0:256]).then_inc(mid, 1)
            nc.vector.tensor_copy(hh[:, 1, P:D], pb[5][:, 256:384]).then_inc(mid, 1)
            nc.vector.memset(bd, 0.0).then_inc(mid, 1)
            dve.wait_ge(mid, 3)
            for h in range(2):
                o_ = h * DH
                nc.vector.tensor_copy(bd[o_:o_ + DH, :, o_:o_ + DH], pb[4][o_:o_ + DH, :].rearrange(
                    "p (h d) -> p h d", h=4)[:, :, o_:o_ + DH]).then_inc(mid, 1)
            dve.wait_ge(S["mid_p"], 1)
            nc.vector.tensor_copy(hh[:, 1, 0:P], pb[7][:, 0:P]).then_inc(mid, 1)
            dve.wait_ge(S["mid_p"], 2)
            for b in range(2):
                nc.vector.tensor_copy(r_m[:, 2 * b:2 * b + 2, :], pb[2 + b][:, :].rearrange(
                    "p (h n) -> p h n", h=2)).then_inc(mid, 1)
            dve.wait_ge(S["mid_p"], 3)
            nc.vector.tensor_scalar(mp[:, :, 0:D], pb[6][:, :].rearrange("p (c n) -> p c n", c=2),
                                    BETA / N, None, ALU.mult).then_inc(mid, 1)
            dve.wait_ge(S["mid_p"], 4)
            nc.vector.tensor_scalar(mp[:, :, D:2 * D], pb[7][:, :].rearrange("p (c n) -> p c n", c=2),
                                    1.0 / N, None, ALU.mult).then_inc(mid, 1)
            nc.vector.memset(w5, 1.0).then_inc(mid, 1)
            dve.wait_ge(mid, 11)

        def pe_mid(pe):
            pe.wait_ge(S["mid_w"], 48)
            pe.wait_ge(S["mid_d"], 5)
            nc.tensor.transpose(pb[7][:, 0:P], hh[:, 0, P:D], ident[:, :]).then_inc(S["mid_p"], 1)
            for h in range(4):
                last = nc.tensor.matmul(pb[2 + h // 2][:, (h % 2) * D:(h % 2) * D + D], bd[:, h, :],
                                        wo_m[:, h, :], start=True, stop=True)
            last.then_inc(S["mid_p"], 1)
            pe.wait_ge(S["mid_d"], 6)
            for m in range(2):
                for c in range(2):
                    last = nc.tensor.matmul(pb[6][:, m * D:m * D + D], hh[:, c, m * P:m * P + P],
                                            wv_m[:, c, :], start=(c == 0), stop=(c == 1))
            last.then_inc(S["mid_p"], 1)
            pe.wait_ge(S["mid_d"], 8)
            for m in range(2):
                for h in range(4):
                    last = nc.tensor.matmul(pb[7][:, m * D:m * D + D], wq_m[:, h, m * P:m * P + P],
                                            r_m[:, h, :], start=(h == 0), stop=(h == 3))
            last.then_inc(S["mid_p"], 1)
            pe.wait_ge(S["mid_d"], 11)

        def sp_a(sp, j, s, last=False):
            for t in range(2):
                wait(sp, S["y"], 6 * j - 6)
                stand(sp)
                full = not (last and t == 1)
                if not full:
                    sp.wait_ge(S["xfpad"], 1)
                rows = P if full else LAST
                sp.dma_start(xf[0:rows, 2 * s + t, :], x[ds((2 * j + t) * P, rows), :]).then_inc(
                    S[f"xf{2 * s + t}"], 16)

        def act_a_scale(act, j, it, s):
            wait(act, S["ttr"], 2 * j)
            for t in range(2):
                act.wait_ge(S[f"xf{2 * s + t}"], it * 16 + 16)
                nc.scalar.activation(tf[:, t, :], xf[:, 2 * s + t, :], ACT.Identity,
                                     scale=c_[:, ds(2 * j + t, 1)],
                                     bias=cb[:, ds(2 * j + t, 1)]).then_inc(S["tf"], 1)

        def pe_a_transpose(pe, j):
            for t in range(2):
                pe.wait_ge(S["tf"], 2 * j + t + 1)
                wait(pe, S["vv"], 4 * j)
                for c in range(2):
                    last = nc.tensor.transpose(pb[2][:, t * 256 + c * P:t * 256 + c * P + P],
                                               tf[:, t, c * P:c * P + P], ident[:, :])
                last.then_inc(S["ttr"], 1)

        def act_a_transposed(act, j):
            wait(act, S["p12"], 2 * j)
            for t in range(2):
                act.wait_ge(S["ttr"], 2 * j + 2)
                nc.scalar.activation(ttf[:, t, :], pb[2][:, t * 256:t * 256 + 256],
                                     ACT.Copy).then_inc(S["ttf"], 1)

        def dve_a_sum(dve, j, groups):
            wait(dve, S["p12"], 2 * j)
            if groups is not None:
                wait(dve, S["acc"], groups)
            for t in range(2):
                dve.wait_ge(S["ttf"], 2 * j + t + 1)
                nc.vector.tensor_tensor(ag[:, t, :].rearrange("p (c n) -> p c n", c=2),
                                        ttf[:, t, :].rearrange("p (c n) -> p c n", c=2),
                                        zT[:, :, ds((2 * j + t) * P, P)], ALU.add).then_inc(S["ag"], 1)

        def pe_a_local(pe, j, t):
            pe.wait_ge(S["ag"], 2 * j + t + 1)
            pe.wait_ge(S["ttf"], 2 * j + 2)
            for c in range(2):
                nc.tensor.matmul(pb[2][:, t * D:t * D + D], ag[:, t, c * P:c * P + P], wg[:, c, :],
                                 start=(c == 0), stop=(c == 1))

        def pe_a_global(pe, j, t):
            wait(pe, S["y"], 6 * j - 4)
            for c in range(2):
                last = nc.tensor.matmul(pb[3 + t][:, :], ttf[:, t, c * P:c * P + P], mp[:, c, :],
                                        start=(c == 0), stop=(c == 1))
            last.then_inc(S["p12"], 1)

        def dve_a_v(dve, j):
            for t in range(2):
                n = 2 * j + t
                dve.wait_ge(S["p12"], 2 * j + 2)
                wait(dve, S["rr"], 2 * j)
                nc.vector.scalar_tensor_tensor(vv[:, t, :], bB[:, :], dsq[:, ds(n, 1)], pb[2][:, t * D:t * D + D],
                                               ALU.mult, ALU.add).then_inc(S["vv"], 1)
                dve.wait_ge(S["vv"], 2 * n + 1)
                nc.vector.scalar_tensor_tensor(vv[:, t, :], pb[3 + t][:, 0:D], deg[:, ds(n, 1)], vv[:, t, :],
                                               ALU.mult, ALU.add).then_inc(S["vv"], 1)

        def act_a_relu(act, j):
            wait(act, S["y"], 6 * j)
            for t in range(2):
                n = 2 * j + t
                act.wait_ge(S["vv"], 2 * n + 2)
                nc.scalar.activation(rr[:, t, :], vv[:, t, :], ACT.Relu).then_inc(S["rr"], 1)
                act.wait_ge(S["rr"], n + 1)
                wait(act, S["ssq"], n)
                nc.scalar.activation(sqf, rr[:, t, :], ACT.Square,
                                     accum_out=ss[:, t:t + 1]).then_inc(S["ssq"], 1)

        NCOLS = 24
        NST = 12

        def dve_a_y1(dve, j, s):
            V, st, y = nc.vector, S["st"], S["y"]
            dve.wait_ge(S["ssq"], 2 * j + 2)
            V.tensor_tensor(lo, ss, tiny2[:, ds(j * 2, 2)], ALU.max).then_inc(st, 1)
            wait(dve, S["oo"], 2 * j - 2)
            for t in range(2):
                V.scalar_tensor_tensor(yy[:, s, t, :], pb[3 + t][:, D:2 * D], q[:, ds(2 * j + t, 1)],
                                       xf[:, 2 * s + t, :], ALU.mult, ALU.add).then_inc(y, 1)
            for t in range(2):
                dve.wait_ge(y, 6 * j + 1 + t)
                V.tensor_tensor(yy[:, s, t, :], yy[:, s, t, :], boB[:, :], ALU.add).then_inc(y, 1)

        def dve_a_y2(dve, j, s):
            V, st, y, b0 = nc.vector, S["st"], S["y"], NST * j
            dve.wait_ge(S["rs"], 4 * j + 2)
            dve_polish(dve, lo, rs0, nt_, inv, st, b0 + 1)
            dve.wait_ge(y, 6 * j + 4)
            for t in range(2):
                V.scalar_tensor_tensor(yy[:, s, t, :], rr[:, t, :], inv[:, t:t + 1], yy[:, s, t, :],
                                       ALU.mult, ALU.add).then_inc(y, 1)

        def dve_a_stats(dve, j, s):
            V, st, y, b0 = nc.vector, S["st"], S["y"], NST * j
            for t in range(2):
                dve.wait_ge(y, 6 * j + 5 + t)
                V.bn_stats(bnf[:, t, :], yy[:, s, t, :]).then_inc(st, 1)
            dve.wait_ge(st, b0 + 6)
            stand(dve)
            for t in range(2):
                V.bn_aggr(mvf[:, t, :], bnf[:, t, :]).then_inc(st, 1)
            dve.wait_ge(st, b0 + 8)
            V.tensor_scalar(vr, mvf[:, :, 1], EPS_LN, None, ALU.add).then_inc(st, 1)

        def dve_a_y3(dve, j):
            dve.wait_ge(S["rs"], 4 * j + 4)
            wait(dve, S["u"], 2 * j)
            dve_polish(dve, vr, rs1, nt_, rstd, S["st"], NST * j + 9)
            nc.vector.scalar_tensor_tensor(nb_, mvf[:, :, 0], -1.0, rstd, ALU.mult, ALU.mult).then_inc(S["nb"], 1)

        def act_a_norm1(act, j):
            act.wait_ge(S["st"], NST * j + 1)
            nc.scalar.activation(rs0, lo, ACT.Ln, scale=2.0 ** 20).then_inc(S["rs"], 1)
            act.wait_ge(S["rs"], 4 * j + 1)
            nc.scalar.activation(rs0, rs0, ACT.Exp, scale=-0.5, bias=lnb[:, :]).then_inc(S["rs"], 1)

        def act_a_norm2(act, j):
            act.wait_ge(S["st"], NST * j + 9)
            nc.scalar.activation(rs1, vr, ACT.Ln).then_inc(S["rs"], 1)
            act.wait_ge(S["rs"], 4 * j + 3)
            nc.scalar.activation(rs1, rs1, ACT.Exp, scale=-0.5).then_inc(S["rs"], 1)

        def act_a_u(act, j, s):
            wait(act, S["tru"], j)
            act.wait_ge(S["nb"], j + 1)
            for t in range(2):
                nc.scalar.activation(uu[:, t, :], yy[:, s, t, :], ACT.Identity, scale=rstd[:, t:t + 1],
                                     bias=nb_[:, t:t + 1]).then_inc(S["u"], 1)

        def pe_b_transpose(pe, j):
            pe.wait_ge(S["u"], 2 * j + 2)
            wait(pe, S["h2w"], 2 * j)
            for t in range(2):
                for c in range(2):
                    last = nc.tensor.transpose(pb[5][:, c * 256 + t * P:c * 256 + t * P + P],
                                               uu[:, t, c * P:c * P + P], ident[:, :])
            last.then_inc(S["tru"], 1)

        def act_b_transposed(act, j):
            act.wait_ge(S["tru"], j + 1)
            wait(act, S["h1"], 6 * j)
            nc.scalar.activation(uT, pb[5][:, :].rearrange("p (c n) -> p c n", c=2),
                                 ACT.Copy).then_inc(S["ut"], 1)

        H1PS = [pb[b][:, h * 256:h * 256 + 256] for b in (6, 7, 6) for h in range(2)]
        H2PS = [pb[7][:, 0:256], pb[7][:, 256:512], pb[6][:, 0:256]]
        WBPS = [pb[5][:, 0:256], pb[5][:, 256:512]]
        OPS = [pb[7][:, 0:256], pb[7][:, 256:512]]
        GPS = pb[5][:, 0:8].rearrange("p (t e) -> p t e", t=2)
        WTPS = pb[5][0:R9, 0:256]

        def pe_b_gates(pe, j):
            pe.wait_ge(S["ut"], j + 1)
            for t in range(2):
                for c in range(2):
                    last = nc.tensor.matmul(GPS[:, t, :], uT[:, c, t * P:t * P + P], gw[:, c, :],
                                            start=(c == 0), stop=(c == 1))
            last.then_inc(S["gates"], 1)

        def pe_b_first(pe, j, ms):
            for m in ms:
                if m == 0:
                    wait(pe, S["oo"], 2 * j)
                if m == 4:
                    pe.wait_ge(S["h1e"], 6 * j + 2)
                for c in range(2):
                    last = nc.tensor.matmul(H1PS[m], w1[:, c, m, :], uT[:, c, :],
                                            start=(c == 0), stop=(c == 1))
                last.then_inc(S["h1"], 1)

        def act_b_first(act, j, ms):
            for m in ms:
                act.wait_ge(S["h1"], 6 * j + m // 2 * 2 + 2)
                if m == 0:
                    wait(act, S["h2"], 3 * j)
                nc.scalar.activation(h1[:, m, :], H1PS[m], ACT.Relu, bias=hb[:, m:m + 1]).then_inc(S["h1e"], 1)

        NGATE = 21

        def dve_b_gate1(dve, j):
            ga = S["gap"]
            dve.wait_ge(S["gates"], j + 1)
            nc.vector.tensor_tensor(lg, GPS, gbB[:, :].rearrange("p (t e) -> p t e", t=2),
                                    ALU.add).then_inc(ga, 1)
            dve.wait_ge(ga, NGATE * j + 1)
            nc.vector.tensor_reduce(v2[0], lg, AX, ALU.max).then_inc(ga, 1)
            dve.wait_ge(ga, NGATE * j + 2)
            nc.vector.tensor_tensor(lg, lg, v2[0].unsqueeze(2).to_broadcast([P, 2, 4]),
                                    ALU.subtract).then_inc(ga, 1)

        def act_b_gate1(act, j):
            act.wait_ge(S["gap"], NGATE * j + 3)
            nc.scalar.activation(e_g, lg, ACT.Exp).then_inc(S["eg"], 1)

        def dve_b_gate2(dve, j):
            ga = S["gap"]
            n = [3]

            def chain(ins):
                ins.then_inc(ga, 1)
                n[0] += 1
                dve.wait_ge(ga, NGATE * j + n[0])

            V = nc.vector
            rk = rank[:, :].rearrange("p (t e) -> p t e", t=2)

            def bc(v):
                return v.unsqueeze(2).to_broadcast([P, 2, 4])

            dve.wait_ge(S["eg"], j + 1)
            chain(V.tensor_reduce(v2[1], e_g, AX, ALU.add))
            chain(V.reciprocal(v2[2], v2[1]))
            chain(V.tensor_tensor(gt, e_g, bc(v2[2]), ALU.mult))
            chain(V.tensor_reduce(v2[3], gt, AX, ALU.max))
            chain(V.tensor_tensor(t8, gt, bc(v2[3]), ALU.is_equal))
            chain(V.tensor_tensor(t8, t8, rk, ALU.mult))
            chain(V.tensor_reduce(v2[4], t8, AX, ALU.max))
            chain(V.tensor_tensor(o1, rk, bc(v2[4]), ALU.is_equal))
            chain(V.scalar_tensor_tensor(g2, o1, -4.0, gt, ALU.mult, ALU.add))
            chain(V.tensor_reduce(v2[5], g2, AX, ALU.max))
            V.tensor_tensor(v2[7], v2[5], v2[3], ALU.subtract).then_inc(S["lg"], 1)
            chain(V.tensor_tensor(t8, g2, bc(v2[5]), ALU.is_equal))
            chain(V.tensor_tensor(t8, t8, rk, ALU.mult))
            chain(V.tensor_reduce(v2[6], t8, AX, ALU.max))
            chain(V.tensor_tensor(o2, rk, bc(v2[6]), ALU.is_equal))
            assert n[0] == NGATE - 4

        def act_b_gate2(act, j):
            act.wait_ge(S["lg"], j + 1)
            nc.scalar.activation(v2[8], v2[7], ACT.Exp).then_inc(S["ed"], 1)

        def dve_b_gate3(dve, j):
            ga = S["gap"]
            V = nc.vector

            def bc(v):
                return v.unsqueeze(2).to_broadcast([P, 2, 4])

            dve.wait_ge(S["ed"], j + 1)
            V.tensor_scalar(v2[11], v2[8], 1.0, None, ALU.add).then_inc(ga, 1)
            dve.wait_ge(ga, NGATE * j + NGATE - 3)
            V.reciprocal(v2[9], v2[11]).then_inc(ga, 1)
            dve.wait_ge(ga, NGATE * j + NGATE - 2)
            V.tensor_tensor(o1, o1, bc(v2[9]), ALU.mult).then_inc(ga, 1)
            V.tensor_tensor(v2[10], v2[8], v2[9], ALU.mult).then_inc(ga, 1)
            dve.wait_ge(ga, NGATE * j + NGATE)
            V.tensor_tensor(o2, o2, bc(v2[10]), ALU.mult).then_inc(S["w5"], 1)
            dve.wait_ge(S["w5"], 6 * j + 1)
            V.tensor_tensor(w5[:, :, 0:4], o1, o2, ALU.add).then_inc(S["w5"], 1)
            dve.wait_ge(S["w5"], 6 * j + 2)
            wait(dve, S["wt"], j)

            def thrice(v):
                return v.unsqueeze(2).to_broadcast([P, 2, 3, 5])

            V.tensor_copy(w9[:, :, 0], thrice(w5)).then_inc(S["w5"], 1)
            dve.wait_ge(S["w5"], 6 * j + 3)
            V.tensor_tensor(w5r, w5, w9[:, :, 0, 0], ALU.subtract).then_inc(S["w5"], 1)
            dve.wait_ge(S["w5"], 6 * j + 4)
            V.tensor_copy(w9[:, :, 1], thrice(w5r)).then_inc(S["w5"], 1)
            dve.wait_ge(S["w5"], 6 * j + 5)
            V.tensor_tensor(w9[:, :, 2], thrice(w5r), w9[:, :, 1], ALU.subtract).then_inc(S["w5"], 1)

        def pe_b_weights(pe, j):
            pe.wait_ge(S["w5"], 6 * j + 6)
            for t in range(2):
                last = nc.tensor.matmul(WTPS[:, t * P:t * P + P], w9[:, t].rearrange("p i j e -> p (i j e)"),
                                        ident_b[:, :], start=True, stop=True)
            last.then_inc(S["wt"], 1)

        def dve_b_weights(dve, j):
            dve.wait_ge(S["wt"], j + 1)
            wait(dve, S["pout"], 2 * j)
            nc.vector.tensor_copy(wT[0:R9, :], WTPS).then_inc(S["wtc"], 1)

        def pe_b_second(pe, j):
            pe.wait_ge(S["wtc"], j + 1)
            for r in range(2):
                last = nc.tensor.matmul(WBPS[r], pick_b[:, r, :], wT[0:R9, :], start=True, stop=True)
            last.then_inc(S["wb"], 1)
            pe.wait_ge(S["h1e"], 6 * j + 4)
            for c in range(2):
                last = nc.tensor.matmul(H2PS[0], w2s[:, c, :], h1[:, c, :], start=(c == 0), stop=(c == 1))
            last.then_inc(S["h2"], 1)

        def pe_b_second_experts(pe, j):
            pe.wait_ge(S["h1e"], 6 * j + 6)
            for r in range(2):
                for e in range(2):
                    last = nc.tensor.matmul(H2PS[1 + r][e * 64:e * 64 + 64, :], w2e[:, 2 * r + e, :],
                                            h1[:, 2 + 2 * r + e, :], start=True, stop=True)
                last.then_inc(S["h2"], 1)

        def act_b_second(act, j):
            wait(act, S["pout"], 2 * j)
            for m in range(3):
                act.wait_ge(S["h2"], 3 * j + max(m, 1) + 1)
                nc.scalar.activation(h2[:, m, :], H2PS[m], ACT.Relu, bias=hb[:, 6 + m:7 + m]).then_inc(S["h2e"], 1)

        def dve_b_second(dve, j):
            dve.wait_ge(S["wb"], j + 1)
            for r in range(2):
                dve.wait_ge(S["h2e"], 3 * j + 2 + r)
                nc.vector.tensor_tensor(h2[:, 1 + r, :], h2[:, 1 + r, :], WBPS[r], ALU.mult).then_inc(S["h2w"], 1)

        def pe_b_out(pe, j):
            pe.wait_ge(S["h2e"], 3 * j + 3)
            pe.wait_ge(S["h2w"], 2 * j + 2)
            for t in range(2):
                o_ = t * P
                nc.tensor.matmul(OPS[t], h2[:, 0, o_:o_ + P], w3[:, 0, :], start=True, stop=False)
                nc.tensor.matmul(OPS[t], wT[0:R9, o_:o_ + P], ob9[:, :], start=False, stop=False)
                for r in range(2):
                    last = nc.tensor.matmul(OPS[t], h2[:, 1 + r, o_:o_ + P], w3[:, 1 + r, :],
                                            start=False, stop=(r == 1))
                last.then_inc(S["pout"], 1)

        def dve_b_out(dve, j, it, s):
            wait(dve, S[f"st{s}"], it * 32)
            for t in range(2):
                dve.wait_ge(S["pout"], 2 * j + 2)
                nc.vector.tensor_tensor(oo[:, s, t, :], yy[:, s, t, :], OPS[t], ALU.add).then_inc(S["oo"], 1)

        def sp_b_out(sp, j, s, last=False):
            for t in range(2):
                sp.wait_ge(S["oo"], 2 * j + t + 1)
                stand(sp)
                rows = LAST if last and t == 1 else P
                sp.dma_start(out[ds((2 * j + t) * P, rows), :], oo[0:rows, s, t, :]).then_inc(S[f"st{s}"], 16)

        g_row_i = arena[:, 5400:5528].bitcast(I32)
        g_row, g_cmp = arena[:, 5528:5656], arena[:, 5656:5784]
        g_eq = arena[:, 5784:5848].bitcast(BF16)
        g_sum, g_z = arena[:, 5848:6104], arena[:, 6104:6360]
        g_dst, g_cnt, g_tgt = arena[:, 6360:6361], arena[:, 6361:6362], arena[:, 6362:6363]
        g_tgt_i = arena[:, 6363:6364].bitcast(I32)
        trash, low = arena[:, 6364:6365], arena[:, 6400:6528]
        free = zflat[:, 18000:18000 + 4 * ET]
        g_hi_i, g_lo_i = free[:, 0:ET].bitcast(I32), free[:, ET:2 * ET].bitcast(I32)
        g_hi, g_lo = free[:, 2 * ET:3 * ET], free[:, 3 * ET:4 * ET]
        GD = 11
        g_oha = G[:, 0:4, :].rearrange("p k f -> p (k f)")[:, 0:GD * P].rearrange("p (k n) -> p k n", k=GD)
        g_ohb = G[:, 4:8, :].rearrange("p k f -> p (k f)")[:, 0:GD * P].rearrange("p (k n) -> p k n", k=GD)
        deg_dram = nc.dram_tensor("deg_dram", (1, DA * P * LB), F32, kind="Internal").ap()

        def tiles_in_pairs(engine, step):
            step(0, 0, 0)
            step(1, 0, 1)
            with engine.Fori(1, NP - 1) as it:
                step(it * 2, it, 0)
                step(it * 2 + 1, it, 1)
            step(NT - 2, NP - 1, 0)
            step(NT - 1, NP - 1, 1)

        def pairs_with_groups(engine, step):
            step(0, 0, 0)
            step(1, 0, 1)
            with engine.Fori(1, NPL // 2 - 1) as it:
                step(it * 2, it, 0)
                step(it * 2 + 1, it, 1)
            step(NPL - 2, NPL // 2 - 1, 0)
            step(NPL - 1, NPL // 2 - 1, 1)

        def pairs_alone(engine, step):
            step(0, 0, 0)
            step(1, 0, 1)
            with engine.Fori(1, NP // 2 - 1) as it:
                step(it * 2, it, 0)
                step(it * 2 + 1, it, 1)
            for j in range(NP - 3, NP):
                step(j, j // 2, j % 2)

        def group_at(j, it, s, n):
            return j * GPP + (GP1 + n), it * GPP + (GP1 + GPP * s + n) // 2, (GPP * s + n) % 2

        def choose(engine, fast, general):
            engine.wait_ge(S["flag"], 1)
            f = engine.value_load(flag_i[0:1, 0:1], min_val=0, max_val=1)
            with engine.If(f == 0):
                fast()
            with engine.Else():
                general()

        NSPLIT = 6

        def constant(i, value):
            return isinstance(i, int) and i == value

        block = ctx.enter_context(nc.Block())

        a_var, a_gd, a_gs, a_gn, a_di, a_sd, a_rn, a_m, a_t = (
            arena[:, 8700 + 100 * k:8700 + 100 * k + NT] for k in range(9))

        @block.sync
        def _(sp):
            sp.dma_start(dst_i, dst_t).then_inc(S["dst"], 16)
            for to, of in ((lim, c_limit), (ident[:, :], c_ident), (iota[:, :], c_iota.to_broadcast([P, P])),
                           (rank[:, :], c_rank.to_broadcast([P, 8]))):
                sp.dma_start(to, of).then_inc(S["const"], 16)

            def load_chunk(c, it, s):
                wait(sp, S[f"xuse{s}"], it)
                stand(sp)
                sp.dma_start(xc[:, s, :, :], x[ds(c * (CH * P), CH * P), :].rearrange(
                    "(k p) d -> p k d", p=P)).then_inc(S[f"xin{s}"], 16)

            def reload_chunk(c, s):
                if constant(c, 0) or constant(c, 1):
                    sp.wait_ge(S[f"xuse{s}"], NCH // 2)
                else:
                    sp.wait_ge(S["t_ra"], c * T_ACT - T_ACT)
                    sp.wait_ge(S["t_rp"], c * (CH - T_ACT) - (CH - T_ACT))
                stand(sp)
                if constant(c, NCH - 1):
                    load_last()
                else:
                    sp.dma_start(xc[:, s, :, :], x[ds(c * (CH * P), CH * P), :].rearrange(
                        "(k p) d -> p k d", p=P)).then_inc(S[f"xin{s}"], 16)

            def load_last():
                c = NCH - 1
                sp.dma_start(xc[:, 1, 0:CH - 1, :], x[c * CH * P:c * CH * P + (CH - 1) * P, :].rearrange(
                    "(k p) d -> p k d", p=P)).then_inc(S["xin1"], 16)
                sp.dma_start(xc[0:LAST, 1, CH - 1, :], x[(NT - 1) * P:N, :]).then_inc(S["xin_last"], 16)

            load_chunk(0, 0, 0)
            load_chunk(1, 0, 1)
            with sp.Fori(1, NCH // 2 - 1) as it:
                load_chunk(it * 2, it, 0)
                load_chunk(it * 2 + 1, it, 1)
            load_chunk(NCH - 2, NCH // 2 - 1, 0)
            loads = ((wkv[:, :, :], w_kvT.rearrange("(c p) n -> p c n", p=P)),
                     (wg[:, :, :], w_gcn.rearrange("(c p) n -> p c n", p=P)),
                     (bB[:, :], b_gcn.to_broadcast([P, D])), (boB[:, :], b_out.to_broadcast([P, D])),
                     (gbB[:, 0:4], gb.to_broadcast([P, 4])), (gbB[:, 4:8], gb.to_broadcast([P, 4])),
                     (hb[:, :], h_bias), (ob[:, :], o_bias), (pick[:, :, :], c_pick), (parts[:, :], c_parts),
                     (w1[:, :, 0:2, :], sW1.rearrange("(c p) (m n) -> p c m n", p=P, m=2)),
                     (w1[:, 0, 2:6, :], eW1[:, 0:P, :].rearrange("e p n -> p e n")),
                     (w1[:, 1, 2:6, :], eW1[:, P:D, :].rearrange("e p n -> p e n")),
                     (w2s[:, :, :], sW2.rearrange("(c p) n -> p c n", p=P)),
                     (w2e[:, :, :], eW2.rearrange("e p n -> p e n")),
                     (w3[:, 0, :], sW3), (w3[:, 1:3, :], eW3.rearrange("(r p) n -> p r n", p=P)),
                     (gw[:, :, :], gW.rearrange("(c p) n -> p c n", p=P)))
            assert len(loads) == NWEIGHTS
            for to, of in loads:
                sp.dma_start(to, of).then_inc(S["weights"], 16)
            sp.wait_ge(S["xpad"], 1)
            load_last()

            def degrees():
                sp.wait_ge(S["deg_q"], 1)
                sp.dma_start(deg_dram.rearrange("o (a p l) -> (o p) a l", p=P, l=LB),
                             deg_q.rearrange("p (a l) -> p a l", l=LB)).then_inc(S["deg_row"], 16)
                sp.wait_ge(S["deg_row"], 16)
                sp.dma_start(deg_98, deg_dram[:, 0:NPAD].rearrange("o (n p) -> (o n) p", p=P)).then_inc(
                    S["deg_98"], 16)

            choose(sp, degrees, lambda: sp.nop())

            def store_chunk(c, s):
                sp.wait_ge(S["t_lo"], c + 1)
                stand(sp)
                sp.dma_start(table[ds(c * (CH * P), CH * P), :].rearrange("(k p) f -> p k f", p=P),
                             tb[:, s, :, :]).then_inc(S[f"t_out{s}"], 16)

            for c in range(3):
                reload_chunk(c, c % 2)
            with sp.Fori(0, NCH // 2 - 2) as it:
                for s in range(2):
                    reload_chunk(it * 2 + (s + 3), 1 - s)
                    store_chunk(it * 2 + s, s)
            reload_chunk(NCH - 1, 1)
            for c in range(NCH - 4, NCH):
                store_chunk(c, c % 2)
            sp.wait_ge(S["t_out0"], 16 * (NCH // 2))
            sp.wait_ge(S["t_out1"], 16 * (NCH // 2))
            sp.nop().then_inc(S["t_done"], 1)

            def load_kv(i, s):
                if not constant(i, NT - 2) and not constant(i, NT - 1):
                    sp_kv_x(sp, i + 2, s, constant(i, NT - 3))

            def pairs_end(j):
                if j + 2 < NP:
                    sp_a(sp, j + 2, j % 2, j + 2 == NP - 1)
                sp_b_out(sp, j - 1, (j - 1) % 2)

            def fast():
                for s in range(2):
                    sp_group_idx(sp, s, 0, s)
                    sp_kv_x(sp, s, s)

                def step(i, it, s):
                    load_kv(i, s)
                    sp_group_idx(sp, i + 2, it + 1, s)

                step(0, 0, 0)
                step(1, 0, 1)
                with sp.Fori(1, NP - 2) as it:
                    step(it * 2, it, 0)
                    step(it * 2 + 1, it, 1)
                for i in range(NT - 4, NT):
                    step(i, i // 2, i % 2)
                sp_mid(sp)
                sp.wait_ge(S["mid_d"], 11)
                sp_a(sp, 0, 0)
                sp_a(sp, 1, 1)

                def pair(j, it, s):
                    sp_a(sp, j + 2, s)
                    for n in range(GPP):
                        g, turn, slot = group_at(j, it, s, n)
                        sp_group_idx(sp, g + 2, turn + 1, slot)
                        if n == 0 and not constant(j, 0):
                            sp_b_out(sp, j - 1, 1 - s)

                pair(0, 0, 0)
                pair(1, 0, 1)
                with sp.Fori(1, NPL // 2 - 1) as it:
                    pair(it * 2, it, 0)
                    pair(it * 2 + 1, it, 1)
                for j in (NPL - 2, NPL - 1):
                    sp_a(sp, j + 2, j % 2)
                    for n in range(GPP):
                        g = GP1 + j * GPP + n + 2
                        sp_group_idx(sp, g, g // 2, g % 2, K if g < NG else TAILT)
                        if n == 0:
                            sp_b_out(sp, j - 1, (j - 1) % 2)
                for j in range(NPL, NP):
                    pairs_end(j)
                sp_b_out(sp, NP - 1, (NP - 1) % 2, True)

            def general():
                sp.wait_ge(S["g_zero"], 1)
                for c in range(NCH):
                    sp.dma_start(zsum[c * CH * P:(c + 1) * CH * P, :].rearrange("(k p) d -> p k d", p=P),
                                 tc[:, 0, :, :]).then_inc(S["g_clear"], 16)
                sp.dma_start(zsum[NPAD:NPAD + P, :], tc[:, 0, 0, :]).then_inc(S["g_clear"], 16)
                sp.dma_start(low, c_low).then_inc(S["g_clear"], 16)
                sp.dma_start(trash, c_trash).then_inc(S["g_clear"], 16)

                def tile(i):
                    wait(sp, S["g_sc"], i * 16)
                    stand(sp)
                    sp.dma_start(idx[:, 0, 0:1], src_t[:, ds(i, 1)], allow_slow_non_contiguous=True).then_inc(S["g_idx"], 16)
                    sp.dma_start(idx[:, 0, 1:2], dst_t[:, ds(i, 1)], allow_slow_non_contiguous=True).then_inc(S["g_idx"], 16)
                    sp.dma_start(g_row_i, dst_rows[ds(i, 1), :].to_broadcast([P, P])).then_inc(S["g_idx"], 16)

                tile(0)
                with sp.Fori(1, ET) as i:
                    tile(i)
                sp.wait_ge(S["g_sc"], 16 * ET)

                def back(n):
                    wait(sp, S["g_ztr"], n)
                    stand(sp)
                    sp.dma_start(g_z, zsum[ds(n * P, P), :]).then_inc(S["g_zld"], 16)

                back(0)
                with sp.Fori(1, NT) as n:
                    back(n)
                sp.wait_ge(S["g_ztr"], NT)
                for s in range(2):
                    sp_kv_x(sp, s, s)
                load_kv(0, 0)
                load_kv(1, 1)
                with sp.Fori(1, NP - 2) as it:
                    load_kv(it * 2, 0)
                    load_kv(it * 2 + 1, 1)
                for i in range(NT - 4, NT - 2):
                    load_kv(i, i % 2)
                sp_mid(sp)
                sp.wait_ge(S["mid_d"], 11)
                sp_a(sp, 0, 0)
                sp_a(sp, 1, 1)
                sp_a(sp, 2, 0)
                sp_a(sp, 3, 1)
                sp_b_out(sp, 0, 0)
                with sp.Fori(1, NP // 2 - 1) as it:
                    for s in range(2):
                        sp_a(sp, it * 2 + (s + 2), s)
                        sp_b_out(sp, it * 2 + (s - 1), 1 - s)
                for j in range(NP - 3, NP):
                    pairs_end(j)
                sp_b_out(sp, NP - 1, (NP - 1) % 2, True)

            choose(sp, fast, general)
            sp.wait_ge(S["st0"], 32 * (NP - NP // 2))
            sp.wait_ge(S["st1"], 32 * (NP // 2))

        @block.gpsimd
        def _(pool):
            pool.memset(ones[:, :], 1.0).then_inc(S["consts_made"], 1)
            pool.memset(ones_b[:, :], 1.0).then_inc(S["consts_made"], 1)
            pool.memset(lnb[:, :], 10 * math.log(2.0)).then_inc(S["consts_made"], 1)

            def degrees_add():
                pool.memset(deg_8, 0.0).then_inc(S["deg_zero"], 1)
                pool.wait_ge(S["deg_zero"], 1)

                def add(b, s, n=BG):
                    at_ = first_columns(high_i[0:1, ds(b * BG, n)], mybir.EngineType.Pool, NPAD // LB)
                    pool.wait_ge(S["deg_cp"], b + 1)
                    for k in range(n):
                        wait(pool, S[f"deg_add{k}"], b)
                        win = deg_8[:, k, ds(at_[k], WH)]
                        nc.gpsimd.tensor_tensor(win, win, counts[:, s, k * WH:(k + 1) * WH],
                                                ALU.add).then_inc(S[f"deg_add{k}"], 1)

                add(0, 0)
                add(1, 1)
                with pool.Fori(1, NB // 2) as it:
                    add(it * 2, 0)
                    add(it * 2 + 1, 1)
                add(NB - 1, 0)
                add(NB, 1, 1)

            choose(pool, degrees_add, lambda: pool.nop())

            def scale(c):
                s = c % 2
                pool.wait_ge(S[f"xin{s}"], 16 * (NCH // 2 + c // 2 + 1))
                if c == NCH - 1:
                    pool.wait_ge(S["xin_last"], 32)
                wait(pool, S["t_r1"], c - 1)
                for k in range(T_ACT, CH):
                    n = c * CH + k
                    nc.gpsimd.tensor_scalar(tc[:, s, k, :], xc[:, s, k, :], c_[:, n:n + 1], cb[:, n:n + 1],
                                            ALU.mult, ALU.add).then_inc(S["t_rp"], 1)
                last = pool.memset(zflat[:, 2 * ZN * c // NCH:2 * ZN * (c + 1) // NCH], 0.0)
                last.then_inc(S["zclear"], 1)

            pool.wait_ge(S["cols"], NCOLS)
            for c in range(NCH):
                scale(c)
            pool.wait_ge(S["t_done"], 1)

            def fast():
                for s in range(2):
                    pool_group(pool, s, 0, s)
                with pool.Fori(1, NG // 2) as it:
                    pool_group(pool, it * 2, it, 0)
                    pool_group(pool, it * 2 + 1, it, 1)
                pool_group(pool, NG - 1, NG // 2, 0)
                pool_group(pool, NG, NG // 2, 1, TAILT)

            def general():
                def tile(i):
                    pool.wait_ge(S["g_idx"], i * 48 + 48)
                    wait(pool, S["g_sum"], i)
                    stand(pool)
                    pool.indirect_dma_start(G[:, 0, :], None, table,
                                            bass.IndirectOffsetOnAxis(ap=idx[:, 0, 0:1], axis=0)
                                            ).then_inc(S["g_gat"], 16)
                    pool.wait_ge(S["g_copy"], i + 1)
                    stand(pool)
                    pool.indirect_dma_start(zsum, bass.IndirectOffsetOnAxis(ap=g_tgt_i, axis=0), g_sum, None,
                                            compute_op=ALU.add).then_inc(S["g_sc"], 16)
                    pool.wait_ge(S["g_sc"], i * 16 + 16)

                pool.wait_ge(S["g_clear"], 16 * (NCH + 3))
                tile(0)
                with pool.Fori(1, ET) as i:
                    tile(i)

            choose(pool, fast, general)

        @block.scalar
        def _(act):
            def sums(c, it, s):
                n = [0]

                def step(ins):
                    ins.then_inc(S["ast"], 1)
                    n[0] += 1

                def settle():
                    act.wait_ge(S["ast"], c * (2 * CH + 3) + n[0])

                act.wait_ge(S[f"xin{s}"], it * 16 + 16)
                for k in range(CH):
                    step(nc.scalar.activation(junk[:, k, :], xc[:, s, k, :], ACT.Copy, accum_out=rsum[:, k:k + 1]))
                settle()
                step(nc.scalar.activation(rneg[:, :], rsum[:, :], ACT.Copy, scale=-1.0 / D))
                step(nc.scalar.activation(stat[:, ds(c * CH, CH), 0], rsum[:, :], ACT.Copy, scale=1.0 / D))
                settle()
                for k in range(CH):
                    step(nc.scalar.activation(junk[:, k, :], xc[:, s, k, :], ACT.Square, bias=rneg[:, k:k + 1],
                                              accum_out=rsq[:, k:k + 1]))
                settle()
                act.nop().then_inc(S[f"xuse{s}"], 1)
                step(nc.scalar.activation(stat[:, ds(c * CH, CH), 1], rsq[:, :], ACT.Copy, scale=1.0 / D))
                settle()

            def t_scale(c, it, s):
                act.wait_ge(S[f"xin{s}"], it * 16 + 16 * (NCH // 2) + 16)
                if constant(c, NCH - 1):
                    act.wait_ge(S["xin_last"], 32)
                wait(act, S["t_r1"], c - 1)
                for k in range(T_ACT):
                    n = c * CH + k
                    nc.scalar.activation(tc[:, s, k, :], xc[:, s, k, :], ACT.Identity,
                                         scale=c_[:, ds(n, 1)], bias=cb[:, ds(n, 1)]).then_inc(S["t_ra"], 1)

            def t_first(c, it, s):
                act.wait_ge(S["t_ra"], c * T_ACT + T_ACT)
                act.wait_ge(S["t_rp"], c * (CH - T_ACT) + (CH - T_ACT))
                wait(act, S[f"t_out{s}"], it * 16)
                nc.scalar.activation(tb[:, s, :, 0:D], tc[:, s, :, :], ACT.Copy).then_inc(S["t_hi"], 1)

            def t_second(c, s):
                act.wait_ge(S["t_r1"], c + 1)
                nc.scalar.activation(tb[:, s, :, D:2 * D], rc, ACT.Copy).then_inc(S["t_mid"], 1)

            act.preload_act_table_set("natural_log_exp_and_others")
            sums(0, 0, 0)
            sums(1, 0, 1)
            with act.Fori(1, NCA // 2) as it:
                sums(it * 2, it, 0)
                sums(it * 2 + 1, it, 1)
            sums(NCA - 1, NCA // 2, 0)

            def guess(v, to, scale=1.0, bias=0.0):
                nc.scalar.activation(to, v, ACT.Ln, scale=scale).then_inc(S["colg"], 1)
                n[0] += 1
                act.wait_ge(S["colg"], n[0])
                nc.scalar.activation(to, to, ACT.Exp, scale=-0.5, bias=bias).then_inc(S["colg"], 1)
                n[0] += 1

            n = [0]
            act.wait_ge(S["consts_made"], 3)
            act.wait_ge(S["cols"], 1)
            guess(a_var, a_gs)
            act.wait_ge(S["cols"], 7)
            guess(a_m, a_gn, 2.0 ** 20, lnb[:, :])
            act.wait_ge(S["deg_c"], 1)
            guess(deg[:, :], a_gd)
            act.wait_ge(S["cols"], NCOLS)
            t_scale(0, 0, 0)
            t_first(0, 0, 0)
            t_scale(1, 0, 1)
            t_second(0, 0)
            t_first(1, 0, 1)
            with act.Fori(1, NCH // 2 - 1) as it:
                for s in range(2):
                    t_scale(it * 2 + s, it, s)
                    t_second(it * 2 + (s - 1), 1 - s)
                    t_first(it * 2 + s, it, s)
            for c in (NCH - 2, NCH - 1):
                t_scale(c, c // 2, c % 2)
                t_second(c - 1, (c - 1) % 2)
                t_first(c, c // 2, c % 2)
            t_second(NCH - 1, 1)

            def kv(i, it, s):
                if not constant(i, NT - 1):
                    act_kv_transposed(act, i + 1, 1 - s)
                act_kv(act, i, s)
                if not (constant(i, NT - 1) or constant(i, NT - 2)):
                    act_kv_scale(act, i + 2, it + 1, s)
                act_kv_norm(act, i)

            def pairs_begin():
                act_a_scale(act, 0, 0, 0)
                act_a_transposed(act, 0)
                act_a_scale(act, 1, 0, 1)
                act_a_relu(act, 0)
                act_a_norm1(act, 0)
                act_a_transposed(act, 1)
                act_a_norm2(act, 0)
                act_a_u(act, 0, 0)

            def pair(j, it, s):
                more = not constant(j, NP - 1)
                act_b_transposed(act, j)
                act_b_gate1(act, j)
                if more and not constant(j, NP - 2):
                    act_a_scale(act, j + 2, it + 1, s)
                act_b_gate2(act, j)
                act_b_first(act, j, (0, 1))
                if more:
                    act_a_relu(act, j + 1)
                act_b_first(act, j, (2, 3, 4, 5))
                if more:
                    act_a_norm1(act, j + 1)
                act_b_second(act, j)
                if more:
                    if not constant(j, NP - 2):
                        act_a_transposed(act, j + 2)
                    act_a_norm2(act, j + 1)
                    act_a_u(act, j + 1, 1 - s)

            def keys():
                act.wait_ge(S["zclear"], NCH)
                act_kv_scale(act, 0, 0, 0)
                act_kv_scale(act, 1, 0, 1)
                act_kv_transposed(act, 0, 0)
                tiles_in_pairs(act, kv)
                act.wait_ge(S["mid_d"], 11)
                pairs_begin()

            def fast():
                keys()
                pairs_with_groups(act, pair)
                for j in range(NPL, NP):
                    pair(j, j // 2, j % 2)

            def general():
                keys()
                pairs_alone(act, pair)

            choose(act, fast, general)

        @block.vector
        def _(dve):
            V = nc.vector

            def chain(signal):
                n = [0]

                def run(ins):
                    ins.then_inc(S[signal], 1)
                    n[0] += 1
                    dve.wait_ge(S[signal], n[0])
                return run

            step = chain("base_f")
            dve.wait_ge(S["dst"], 16)
            step(V.tensor_copy(dst_f, dst_i))
            step(V.tensor_copy(base_f, dst_f[0:1, ::K]))
            step(V.tensor_copy(base_i[:, :], base_f))
            step(V.tensor_scalar(high_t, base_i[:, :], LB.bit_length() - 1, None, ALU.logical_shift_right))
            step(V.tensor_copy(high_f, high_t))
            step(V.tensor_copy(high_i[:, :], high_f))
            dve.wait_ge(S["base_b"], 2)
            bases = pb[7][:, 0:NG + 1]
            step(V.tensor_tensor(dst_f[:, 0:NG * K].rearrange("p (g k) -> p g k", k=K),
                                 dst_f[:, 0:NG * K].rearrange("p (g k) -> p g k", k=K),
                                 bases[:, 0:NG].unsqueeze(2).to_broadcast([P, NG, K]), ALU.subtract))
            step(V.tensor_scalar(dst_f[:, NG * K:ET], dst_f[:, NG * K:ET], bases[:, NG:NG + 1], None,
                                 ALU.subtract))
            step(V.tensor_copy(dloc[:, :], dst_f))
            step(V.tensor_reduce(mx[:, 0:1], dst_f, AX, ALU.max))
            step(V.tensor_reduce(mx[:, 1:2], dst_f, AX, ALU.min))
            step(V.tensor_scalar(mx[:, 1:2], mx[:, 1:2], -1.0, None, ALU.mult))
            step(V.tensor_scalar(mx[:, 2:3], mx[:, 0:1], -(W - 1.0), mx[:, 1:2], ALU.add, ALU.max))
            dve.wait_ge(S["const"], 64)
            step(V.tensor_tensor(lim, lim, base_f, ALU.subtract))
            step(V.tensor_reduce(mx[0:1, 3:4], lim, AX, ALU.max))
            V.tensor_tensor(mx[0:1, 2:3], mx[0:1, 2:3], mx[0:1, 3:4], ALU.max).then_inc(S["range_v"], 1)
            dve.wait_ge(S["range_t"], 1)
            step = chain("flag_c")
            step(V.tensor_reduce(mx[0:1, 4:5], pb[7][0:1, 256:256 + P], AX, ALU.max))
            step(V.tensor_scalar(mx[0:1, 5:6], mx[0:1, 4:5], 0.0, None, ALU.is_gt))
            V.tensor_copy(flag_i[:, :], mx[0:1, 5:6]).then_inc(S["flag"], 1)
            V.tensor_copy(iota_w[:, :], iota[:, 0:W]).then_inc(S["iota_w"], 1)
            dve.wait_ge(S["iota_w"], 1)
            dve.wait_ge(S["consts_made"], 3)

            def degrees_onehots():
                step = chain("deg_oh")
                highs = pb[6][:, 0:NG + 1]
                step(V.tensor_scalar(part_i, dst_i, LB - 1, None, ALU.bitwise_and))
                step(V.tensor_copy(lo_b, part_i))
                step(V.tensor_scalar(part_i, dst_i, LB.bit_length() - 1, None, ALU.logical_shift_right))
                step(V.tensor_copy(dst_f, part_i))
                step(V.tensor_tensor(hi_b[:, 0:NG * K].rearrange("p (g k) -> p g k", k=K),
                                     dst_f[:, 0:NG * K].rearrange("p (g k) -> p g k", k=K),
                                     highs[:, 0:NG].unsqueeze(2).to_broadcast([P, NG, K]), ALU.subtract))
                step(V.tensor_scalar(hi_b[:, NG * K:ET], dst_f[:, NG * K:ET], highs[:, NG:NG + 1], None,
                                     ALU.subtract))

                def block(b, s, tiles=BG * K):
                    wait(dve, S["deg_ps"], b - 1)
                    for of, to, n in ((lo_b, oh_lo, LB), (hi_b, oh_hi, WH)):
                        V.tensor_tensor(to[:, s, 0:tiles, :],
                                        of[:, ds(b * (BG * K), tiles)].unsqueeze(2).to_broadcast([P, tiles, n]),
                                        iota_w[:, 0:n].unsqueeze(1).to_broadcast([P, tiles, n]),
                                        ALU.is_equal).then_inc(S["deg_oh"], 1)

                def counted(b, s, n=BG):
                    dve.wait_ge(S["deg_ps"], b + 1)
                    for k in range(BG):
                        wait(dve, S[f"deg_add{k}"], b - 1)
                    V.tensor_copy(counts[:, s, 0:n * WH], pb[s][0:LB, 0:n * WH]).then_inc(S["deg_cp"], 1)

                block(0, 0)
                block(1, 1)
                counted(0, 0)
                with dve.Fori(1, NB // 2) as it:
                    block(it * 2, 0)
                    counted(it * 2 - 1, 1)
                    block(it * 2 + 1, 1)
                    counted(it * 2, 0)
                block(NB - 1, 0)
                counted(NB - 2, 1)
                block(NB, 1, TAILT)
                counted(NB - 1, 0)
                counted(NB, 1, 1)

            def degrees_collect():
                step = chain("deg_sum")
                for k in range(BG):
                    dve.wait_ge(S[f"deg_add{k}"], NB + (k == 0))
                for k in range(1, BG):
                    step(V.tensor_tensor(deg_8[:, 0, :], deg_8[:, 0, :], deg_8[:, k, :], ALU.add))
                dve.wait_ge(S["deg_t"], 1)
                V.tensor_copy(deg_q, pb[6][:, 0:DA * LB]).then_inc(S["deg_q"], 1)

            def degrees_general():
                step = chain("g_ab")
                step(V.tensor_scalar(g_hi_i, dst_i, 7, None, ALU.logical_shift_right))
                step(V.tensor_scalar(g_lo_i, dst_i, 127, None, ALU.bitwise_and))
                step(V.tensor_copy(g_hi, g_hi_i))
                step(V.tensor_copy(g_lo, g_lo_i))

                def onehots(i):
                    wait(dve, S["g_dps"], i)
                    for of, to, n in ((g_hi, g_oha, NT), (g_lo, g_ohb, P)):
                        V.tensor_tensor(to[:, :, 0:n], of[:, ds(i * GD, GD)].unsqueeze(2).to_broadcast([P, GD, n]),
                                        iota[:, 0:n].unsqueeze(1).to_broadcast([P, GD, n]),
                                        ALU.is_equal).then_inc(S["g_oh"], 1)

                onehots(0)
                with dve.Fori(1, ET // GD) as i:
                    onehots(i)

            def pad_rows():
                dve.wait_ge(S["xuse1"], NCH // 2 - 1)
                V.memset(xc[:, 1, CH - 1, :], 0.0).then_inc(S["xpad"], 1)

            def degrees_fast():
                degrees_onehots()
                pad_rows()
                degrees_collect()

            def degrees_other():
                pad_rows()
                degrees_general()

            choose(dve, degrees_fast, degrees_other)

            def stats(c):
                s, n = c % 2, (c - NCA + 1) * CH
                dve.wait_ge(S[f"xin{s}"], c // 2 * 16 + 16)
                for k in range(CH):
                    V.bn_stats(bns[:, k, :], xc[:, s, k, :]).then_inc(S["bn"], 1)
                dve.wait_ge(S["bn"], n)
                stand(dve)
                for k in range(CH):
                    V.bn_aggr(bna[:, k, :], bns[:, k, :]).then_inc(S["bna"], 1)
                dve.wait_ge(S["bna"], n)
                V.tensor_copy(stat[:, c * CH:(c + 1) * CH, :], bna[:, :, :]).then_inc(S[f"xuse{s}"], 1)
                dve.wait_ge(S[f"xuse{s}"], c // 2 + 1)

            for c in range(NCA, NCH):
                if c == NCH - 1:
                    dve.wait_ge(S["xin_last"], 16)
                stats(c)
            dve.wait_ge(S["ast"], NCA * (2 * CH + 3))

            mean, var = stat[:, :, 0], stat[:, :, 1]
            n = [0]

            def step(ins):
                ins.then_inc(S["cols"], 1)
                n[0] += 1
                dve.wait_ge(S["cols"], n[0])

            def polish(v, guess, to):
                dve_polish(dve, v, guess, a_t, to, S["cols"], n[0])
                n[0] += 3

            step(V.tensor_scalar(a_var, var, EPS_LN, None, ALU.add))
            dve.wait_ge(S["colg"], 2)
            polish(a_var, a_gs, a_sd)
            step(V.tensor_tensor(a_t, var, a_sd, ALU.mult))
            step(V.scalar_tensor_tensor(a_t, a_t, float(D), a_sd, ALU.mult, ALU.mult))
            step(V.tensor_scalar(a_m, a_t, EPS_NRM ** 2, None, ALU.max))
            dve.wait_ge(S["colg"], 4)
            polish(a_m, a_gn, a_rn)
            step(V.tensor_tensor(a_m, a_m, a_rn, ALU.mult))

            dve.wait_ge(S["deg_t"], 2)
            V.tensor_scalar(deg[:, :], pb[6][:, 0:NT], 1.0, None, ALU.add).then_inc(S["deg_c"], 1)
            dve.wait_ge(S["deg_c"], 1)
            dve.wait_ge(S["colg"], 6)
            polish(deg[:, :], a_gd, a_di)
            step(V.tensor_tensor(dsq[:, :], deg[:, :], a_di, ALU.mult))
            step(V.tensor_tensor(q[:, :], a_m, dsq[:, :], ALU.mult))
            step(V.tensor_tensor(q2[:, :], q[:, :], q[:, :], ALU.mult))
            step(V.tensor_scalar(q264[:, :], q2[:, :], 1.0 / DH, None, ALU.mult))
            step(V.tensor_scalar(tiny2[:, :], deg[:, :], EPS_NRM ** 2, None, ALU.mult))
            step(V.tensor_tensor(a_t, a_sd, a_rn, ALU.mult))
            step(V.tensor_tensor(c_[:, :], a_t, a_di, ALU.mult))
            step(V.scalar_tensor_tensor(cb[:, :], mean, -1.0, c_[:, :], ALU.mult, ALU.mult))
            step(V.tensor_tensor(cD[:, :], c_[:, :], deg[:, :], ALU.mult))
            step(V.tensor_tensor(cbD[:, :], cb[:, :], deg[:, :], ALU.mult))
            assert n[0] == NCOLS, n[0]

            def rest(c, s):
                dve.wait_ge(S["t_hi"], c + 1)
                wait(dve, S["t_lo"], c)
                V.tensor_tensor(rc, tc[:, s, :, :], tb[:, s, :, 0:D], ALU.subtract).then_inc(S["t_r1"], 1)

            def third(c, s):
                dve.wait_ge(S["t_mid"], c + 1)
                V.tensor_tensor(tb[:, s, :, 2 * D:3 * D], rc, tb[:, s, :, D:2 * D],
                                ALU.subtract).then_inc(S["t_lo"], 1)

            rest(0, 0)
            third(0, 0)
            rest(1, 1)
            third(1, 1)
            with dve.Fori(1, NCH // 2) as it:
                for s in range(2):
                    rest(it * 2 + s, s)
                    third(it * 2 + s, s)
            dve.wait_ge(S["t_lo"], NCH)

            def clear():
                V.memset(bd, 0.0).then_inc(S["zero_l"], 1)
                dve.wait_ge(S["weights"], 16 * NWEIGHTS)
                wh = wkv[:, :, :].rearrange("p c (h d) -> p (c h) d", d=DH)
                wmean = ks[:, 1, 0:32]
                step = chain("wcent")
                step(V.tensor_reduce(wmean, wh, AX, ALU.add))
                step(V.tensor_scalar(wmean, wmean, 1.0 / DH, None, ALU.mult))
                step(V.tensor_tensor(wh, wh, wmean.unsqueeze(2).to_broadcast([P, 32, DH]), ALU.subtract))
                step = chain("split")
                part = ks[0:R9, 0, 0:P].bitcast(BF16)
                step(V.tensor_copy(ident_b[:, :], ident[:, :]))
                step(V.tensor_copy(pick_b[:, :, :], pick[:, :, :]))
                for i in range(3):
                    step(V.tensor_copy(part, ob[:, :]))
                    if i == 0:
                        step(V.tensor_scalar(ob9[:, :], part, parts[:, 0:1], None, ALU.mult))
                    else:
                        step(V.scalar_tensor_tensor(ob9[:, :], part, parts[:, i:i + 1], ob9[:, :], ALU.mult, ALU.add))
                    if i < 2:
                        step(V.tensor_tensor(ob[:, :], ob[:, :], part, ALU.subtract))
                dve.wait_ge(S["zclear"], NCH)

            def pad_kv(i):
                if constant(i, NT - 3):
                    dve.wait_ge(S["td"], 2 * (NT - 2))
                    V.memset(xk[:, 1, :], 0.0).then_inc(S["xkpad"], 1)

            def pad_a(j):
                if constant(j, NP - 3):
                    dve.wait_ge(S["y"], 6 * (NP - 2))
                    V.memset(xf[:, 1, :], 0.0).then_inc(S["xfpad"], 1)

            def pairs_begin(groups):
                dve_a_sum(dve, 0, groups)
                dve_a_v(dve, 0)
                dve_a_y1(dve, 0, 0)
                dve_a_y2(dve, 0, 0)
                dve_a_stats(dve, 0, 0)
                dve_a_y3(dve, 0)
                dve_a_sum(dve, 1, groups)

            def tiles(kv):
                kv(0, 0, 0)
                kv(1, 0, 1)
                with dve.Fori(1, NP - 2) as it:
                    kv(it * 2, it, 0)
                    kv(it * 2 + 1, it, 1)
                for i in range(NT - 4, NT):
                    kv(i, i // 2, i % 2)

            def pair(j, it, s, grouped):
                more = not constant(j, NP - 1)
                g0 = group_at(j, it, s, 0)[0]
                slot = s
                pad_a(j)
                dve_b_gate1(dve, j)
                dve_b_gate2(dve, j)
                dve_b_gate3(dve, j)
                if more:
                    dve_a_v(dve, j + 1)
                if grouped:
                    dve_group_add(dve, g0, slot)
                    dve_onehot(dve, g0 + 2, slot)
                dve_b_weights(dve, j)
                if grouped:
                    dve_group_add(dve, g0 + 1, 1 - slot)
                    dve_onehot(dve, g0 + 3, 1 - slot)
                if more:
                    dve_a_y1(dve, j + 1, 1 - s)
                    dve_a_y2(dve, j + 1, 1 - s)
                dve_b_second(dve, j)
                if more:
                    dve_a_stats(dve, j + 1, 1 - s)
                if grouped:
                    dve_group_add(dve, g0 + 2, slot)
                if more and not constant(j, NP - 2):
                    dve_a_sum(dve, j + 2, g0 + 3 if grouped else None)
                if more:
                    dve_a_y3(dve, j + 1)
                if grouped:
                    dve_onehot(dve, g0 + 4, slot, TAILT if constant(j, NPL - 1) else K)
                dve_b_out(dve, j, it, s)

            def fast():
                clear()
                dve_onehot(dve, 0, 0)

                def kv(i, it, s):
                    dve_onehot(dve, i + 1, 1 - s)
                    pad_kv(i)
                    dve_kv(dve, i, s)
                    dve_group_add(dve, i, s)

                tiles(kv)
                dve_mid(dve)
                dve_onehot(dve, GP1 + 1, (GP1 + 1) % 2)
                pairs_begin(GP1)
                pairs_with_groups(dve, lambda j, it, s: pair(j, it, s, True))
                dve_group_add(dve, NG - 1, 0)
                dve_group_add(dve, NG, 1)
                dve.wait_ge(S["acc"], NG + 1)
                for j in range(NPL, NP):
                    pair(j, j // 2, j % 2, False)

            def general():
                V.memset(tc[:, 0, :, :], 0.0).then_inc(S["g_zero"], 1)
                dve.wait_ge(S["zclear"], NCH)
                dve.wait_ge(S["g_clear"], 16 * (NCH + 3))

                def tile(i):
                    ch = [0]

                    def step(ins):
                        ins.then_inc(S["g_ch"], 1)
                        ch[0] += 1
                        dve.wait_ge(S["g_ch"], i * 7 + ch[0])

                    dve.wait_ge(S["g_idx"], i * 48 + 48)
                    step(V.tensor_copy(g_row, g_row_i))
                    step(V.tensor_copy(g_dst, idx[:, 0, 1:2]))
                    V.tensor_scalar(g_eq, g_row, g_dst, None, ALU.is_equal).then_inc(S["g_e"], 1)
                    step(V.scalar_tensor_tensor(g_cmp, g_row, g_dst, low, ALU.is_equal, ALU.mult))
                    step(V.tensor_reduce(g_cnt, g_cmp, AX, ALU.max))
                    step(V.tensor_tensor(g_tgt, trash, g_dst, ALU.subtract))
                    step(V.scalar_tensor_tensor(g_tgt, g_tgt, g_cnt, g_dst, ALU.mult, ALU.add))
                    step(V.tensor_copy(g_tgt_i, g_tgt))
                    dve.wait_ge(S["g_sum"], i + 1)
                    V.tensor_copy(g_sum, pb[0][:, 0:D]).then_inc(S["g_copy"], 1)

                tile(0)
                with dve.Fori(1, ET) as i:
                    tile(i)

                def back(n):
                    dve.wait_ge(S["g_ztr"], n + 1)
                    V.tensor_copy(zT[:, :, ds(n * P, P)],
                                  pb[1][:, 0:D].rearrange("p (c n) -> p c n", c=2)).then_inc(S["g_zcp"], 1)

                back(0)
                with dve.Fori(1, NT) as n:
                    back(n)
                dve.wait_ge(S["g_zcp"], NT)
                clear()

                def kv(i, it, s):
                    pad_kv(i)
                    dve_kv(dve, i, s)

                tiles(kv)
                dve_mid(dve)
                pairs_begin(None)
                pairs_alone(dve, lambda j, it, s: pair(j, it, s, False))

            choose(dve, fast, general)

        @block.tensor
        def _(pe):
            T = nc.tensor
            pe.wait_ge(S["consts_made"], 3)
            pe.wait_ge(S["base_f"], 2)
            T.matmul(pb[7][:, 0:NG + 1], ones[0:1, :], base_f, start=True, stop=True).then_inc(S["base_b"], 1)
            pe.wait_ge(S["base_f"], 5)
            T.matmul(pb[6][:, 0:NG + 1], ones[0:1, :], high_f, start=True, stop=True).then_inc(S["base_b"], 1)
            pe.wait_ge(S["const"], 64)
            pe.wait_ge(S["range_v"], 1)
            T.transpose(pb[7][0:1, 256:256 + P], mx[:, 2:3], ident[:, :]).then_inc(S["range_t"], 1)

            def degrees_fast():
                def count(b, s, groups=BG, k=K):
                    pe.wait_ge(S["deg_oh"], b * 2 + (NSPLIT + 2))
                    wait(pe, S["deg_cp"], b - 1)
                    for g in range(groups):
                        for j in range(k):
                            last = T.matmul(pb[s][0:LB, g * WH:(g + 1) * WH], oh_lo[:, s, g * K + j, :],
                                            oh_hi[:, s, g * K + j, :], start=(j == 0), stop=(j == k - 1))
                    last.then_inc(S["deg_ps"], 1)

                count(0, 0)
                count(1, 1)
                with pe.Fori(1, NB // 2) as it:
                    count(it * 2, 0)
                    count(it * 2 + 1, 1)
                count(NB - 1, 0)
                count(NB, 1, 1, TAILT)
                pe.wait_ge(S["deg_sum"], BG - 1)
                for a in range(DA):
                    last = T.transpose(pb[6][:, a * LB:(a + 1) * LB], deg_8[:, 0, a * P:(a + 1) * P],
                                       ident[0:LB, 0:LB])
                last.then_inc(S["deg_t"], 1)
                pe.wait_ge(S["deg_98"], 16)
                T.transpose(pb[6][:, 0:NT], deg_98, ident[0:NT, 0:NT]).then_inc(S["deg_t"], 1)

            def degrees_general():
                def count(i):
                    pe.wait_ge(S["g_oh"], i * 2 + 2)
                    for k in range(GD):
                        last = T.matmul(pb[6][:, 0:NT], g_ohb[:, k, :], g_oha[:, k, 0:NT], start=first and k == 0,
                                        stop=False, skip_group_check=True)
                    last.then_inc(S["g_dps"], 1)

                first = True
                count(0)
                first = False
                with pe.Fori(1, ET // GD) as i:
                    count(i)
                pe.wait_ge(S["g_dps"], ET // GD)
                T.nop().then_inc(S["deg_t"], 2)

            choose(pe, degrees_fast, degrees_general)

            def start_sums():
                pe.wait_ge(S["zero_l"], 1)
                pe.wait_ge(S["wcent"], 3)
                for bank in (4, 5):
                    T.matmul(pb[bank][:, :], bd[:, 0, :], wkv[:, 0, 0:INNER], start=True, stop=False,
                             skip_group_check=True).then_inc(S["psum0"], 1)
                pe_kv_transpose(pe, 0, 0)

            def tiles(grouped):
                def kv(i, it, s):
                    if not constant(i, NT - 1):
                        pe_kv_transpose(pe, i + 1, 1 - s)
                    pe_kv(pe, i, s)
                    if not constant(i, 0):
                        pe_dots(pe, i - 1, 1 - s)
                    pe_hth(pe, i, s)
                    if grouped:
                        pe_group(pe, i, it, s)

                tiles_in_pairs(pe, kv)
                pe_dots(pe, NT - 1, 1)

            def pair(j, it, s, grouped):
                more = not constant(j, NP - 1)
                at_ = [group_at(j, it, s, n) for n in range(GPP)]
                if more:
                    pe_a_local(pe, j + 1, 0)
                pe_b_transpose(pe, j)
                if more:
                    pe_a_global(pe, j + 1, 0)
                pe_b_gates(pe, j)
                if grouped:
                    pe_group(pe, *at_[0])
                if more:
                    pe_a_local(pe, j + 1, 1)
                    pe_a_global(pe, j + 1, 1)
                pe_b_first(pe, j, (0, 1))
                if grouped:
                    pe_group(pe, *at_[1])
                pe_b_weights(pe, j)
                pe_b_first(pe, j, (2, 3, 4, 5))
                pe_b_second(pe, j)
                if more and not constant(j, NP - 2):
                    pe_a_transpose(pe, j + 2)
                pe_b_second_experts(pe, j)
                if grouped:
                    pe_group(pe, *at_[2])
                pe_b_out(pe, j)

            def fast():
                start_sums()
                tiles(True)
                pe_mid(pe)
                pe_a_transpose(pe, 0)
                for t in range(2):
                    pe_a_local(pe, 0, t)
                    pe_a_global(pe, 0, t)
                pe_a_transpose(pe, 1)
                pairs_with_groups(pe, lambda j, it, s: pair(j, it, s, True))
                pe_group(pe, NG - 1, NG // 2, 0)
                pe_group(pe, NG, NG // 2, 1, TAILT)
                for j in range(NPL, NP):
                    pair(j, j // 2, j % 2, False)

            def general():
                def tile(i):
                    pe.wait_ge(S["g_gat"], i * 16 + 16)
                    pe.wait_ge(S["g_e"], i + 1)
                    wait(pe, S["g_copy"], i)
                    for part in range(3):
                        last = T.matmul(pb[0][:, 0:D], g_eq, G[:, 0, part * D:part * D + D],
                                        start=(part == 0), stop=(part == 2))
                    last.then_inc(S["g_sum"], 1)

                tile(0)
                with pe.Fori(1, ET) as i:
                    tile(i)

                def back(n):
                    pe.wait_ge(S["g_zld"], n * 16 + 16)
                    wait(pe, S["g_zcp"], n)
                    for c in range(2):
                        last = T.transpose(pb[1][:, c * P:c * P + P], g_z[:, c * P:c * P + P], ident[:, :])
                    last.then_inc(S["g_ztr"], 1)

                back(0)
                with pe.Fori(1, NT) as n:
                    back(n)
                start_sums()
                tiles(False)
                pe_mid(pe)
                pe_a_transpose(pe, 0)
                for t in range(2):
                    pe_a_local(pe, 0, t)
                    pe_a_global(pe, 0, t)
                pe_a_transpose(pe, 1)
                pairs_alone(pe, lambda j, it, s: pair(j, it, s, False))

            choose(pe, fast, general)


def kernel(x, src, dst, L0_gnn_W_gcn, L0_gnn_b_gcn, L0_gnn_W_V, L0_mix_w_qkv, L0_mix_w_out, L0_mix_b_out,
           L0_ffn_sW1, L0_ffn_sb1, L0_ffn_sW2, L0_ffn_sb2, L0_ffn_sW3, L0_ffn_sb3, L0_ffn_eW1, L0_ffn_eb1,
           L0_ffn_eW2, L0_ffn_eb2, L0_ffn_eW3, L0_ffn_eb3, L0_ffn_gW, L0_ffn_gb):
    import concourse.bacc as _bacc
    from concourse.bass_utils import run_bass_kernel_spmd as _run

    def edge_tiles(a, fill):
        a = np.asarray(a)
        whole = a[:NG * GE].reshape(NG, P, K).transpose(1, 0, 2).reshape(P, NG * K)
        tail = np.full(TAILT * P, fill, a.dtype)
        tail[:E - NG * GE] = a[NG * GE:]
        return np.concatenate([whole, tail.reshape(TAILT, P).T], axis=1)

    dst_t = edge_tiles(dst, N)
    limit = np.zeros((1, NG + 1), np.float32)
    for j in range(NPL):
        for n in range(GPP):
            limit[0, GP1 + GPP * j + n] = 2 * P * (j + 2)
    limit[0, GP1 + GPP * NPL:] = 2 * P * (NPL + 2)
    pick = np.zeros((3, 3, 5, 2, P), np.float32)
    which = np.zeros((3, 3, 5, 3), np.float32)
    for i in range(3):
        which[:, i, :, i] = 1.0
    for e in range(4):
        pick[:, 0, e, e // 2, (e % 2) * 64:(e % 2) * 64 + 64] = 1.0
    w_qkv = np.asarray(L0_mix_w_qkv)
    arrays = {
        "x": x, "src_t": edge_tiles(src, 0), "dst_t": dst_t, "dst_rows": dst_t.T,
        "w_kvT": w_qkv[INNER:].T, "w_q": w_qkv[:INNER], "w_oT": np.asarray(L0_mix_w_out).T,
        "w_V": L0_gnn_W_V, "w_gcn": L0_gnn_W_gcn, "b_gcn": np.asarray(L0_gnn_b_gcn)[None],
        "b_out": np.asarray(L0_mix_b_out)[None], "sW1": L0_ffn_sW1, "eW1": L0_ffn_eW1, "sW2": L0_ffn_sW2,
        "eW2": L0_ffn_eW2, "sW3": L0_ffn_sW3, "eW3": np.asarray(L0_ffn_eW3).reshape(4 * 64, D),
        "gW": L0_ffn_gW, "gb": np.asarray(L0_ffn_gb)[None],
        "h_bias": np.concatenate([np.asarray(a).reshape(-1, P) for a in (
            L0_ffn_sb1, L0_ffn_eb1, L0_ffn_sb2, L0_ffn_eb2)], axis=0).T,
        "o_bias": np.tile(np.concatenate([np.asarray(L0_ffn_eb3), np.asarray(L0_ffn_sb3)[None]], axis=0), (9, 1)),
        "c_ident": np.eye(P, dtype=np.float32), "c_iota": np.arange(P, dtype=np.float32)[None],
        "c_rank": np.array([[4, 3, 2, 1, 4, 3, 2, 1]], np.float32), "c_limit": limit, "c_pick": pick.reshape(R9, 2, P),
        "c_parts": which.reshape(R9, 3),
        "c_low": np.tril(np.ones((P, P), np.float32), -1),
        "c_trash": (NPAD + np.arange(P, dtype=np.float32))[:, None],
    }
    nc = _bacc.Bacc("TRN2", target_bir_lowering=False, num_devices=1)
    feed, args = {}, []
    for name, a in arrays.items():
        a = np.ascontiguousarray(a)
        feed[f"in_{name}"] = a
        args.append(nc.dram_tensor(f"in_{name}", a.shape, mybir.dt.from_np(a.dtype), kind="ExternalInput").ap())
    args.append(nc.dram_tensor("out_rows", (N, D), F32, kind="ExternalOutput").ap())
    build(nc, *args)
    return _run(nc, [feed], core_ids=[0]).results[0]["out_rows"]
```
